# Optimizing a Trainium2 kernel written in Bass

```python
import numpy as np
import jax
import jax.numpy as jnp

def _softmax(x, axis=-1):
    return jax.nn.softmax(x, axis=axis)

def _gelu(x):
    return jax.nn.gelu(x, approximate=True)

def _silu(x):
    return jax.nn.silu(x)

def _sigmoid(x):
    return jax.nn.sigmoid(x)

def _layernorm(x, axis=-1, eps=1e-05):
    m = jnp.mean(x, axis=axis, keepdims=True)
    v = jnp.var(x, axis=axis, keepdims=True)
    return (x - m) / jnp.sqrt(v + eps)

def _scatter_add(tgt, idx, src, axis=0):
    return tgt.at[idx].add(src)

def _segment_sum(src, seg, n):
    return jax.ops.segment_sum(src, seg, n)
kernel_name = 'mk_hybrid_d1_jaxref_r4_a3fcd7'

def setup_inputs(seed: int=0):
    np.random.seed(seed)
    _w = jnp.asarray

    def _L0_attn_a_setup():
        import jax, jax.numpy as jnp
        import numpy as np
        B, S, H, NH = (2, 512, 256, 16)
        HD = H // NH
        key = jax.random.key(seed)
        ks = jax.random.split(key, 9)
        w = lambda k: jax.random.normal(k, (H, H), dtype=jnp.float32) * 0.02
        b = lambda k: jax.random.normal(k, (H,), dtype=jnp.float32) * 0.02
        return {'hidden_states': jax.random.normal(ks[0], (B, S, H), dtype=jnp.float32), 'Wq': w(ks[1]), 'bq': b(ks[2]), 'Wk': w(ks[3]), 'bk': b(ks[4]), 'Wv': w(ks[5]), 'bv': b(ks[6]), 'Wo': w(ks[7]), 'bo': b(ks[8])}
    _L0_attn_a_in = _L0_attn_a_setup()

    def _L0_attn_b_setup():
        import jax, jax.numpy as jnp
        import numpy as np
        BATCH, SEQ, D_MODEL = (2, 512, 256)
        D_STATE, D_CONV = (16, 4)
        DT_RANK = 64

        def _forward(x, conv_w, conv_b, x_proj_dt_w, dt_proj_w, dt_proj_b, B_proj_w, C_proj_w, A_log, D_param):
            B, L, D = x.shape
            xc = jax.lax.conv_general_dilated(x.transpose(0, 2, 1), conv_w, window_strides=(1,), padding=[(D_CONV - 1, 0)], feature_group_count=D, dimension_numbers=('NCH', 'OIH', 'NCH'))
            xc = jax.nn.silu((xc + conv_b[None, :, None]).transpose(0, 2, 1))
            dt = jax.nn.softplus(xc @ x_proj_dt_w.T @ dt_proj_w.T + dt_proj_b)
            B_ssm = xc @ B_proj_w.T
            C_ssm = xc @ C_proj_w.T
            A = -jnp.exp(A_log)
            dA = jnp.exp(dt[..., None] * A)
            dBx = dt[..., None] * B_ssm[:, :, None, :] * xc[..., None]

            def step(h, inp):
                dA_t, dBx_t, C_t = inp
                h = dA_t * h + dBx_t
                y_t = jnp.einsum('bdn,bn->bd', h, C_t)
                return (h, y_t)
            h0 = jnp.zeros((B, D, D_STATE), x.dtype)
            _, ys = jax.lax.scan(step, h0, (dA.transpose(1, 0, 2, 3), dBx.transpose(1, 0, 2, 3), C_ssm.transpose(1, 0, 2)))
            return ys.transpose(1, 0, 2) + D_param * xc
        key = jax.random.key(seed)
        ks = jax.random.split(key, 9)
        x = jax.random.normal(ks[0], (BATCH, SEQ, D_MODEL), jnp.float32)
        conv_w = jax.random.normal(ks[1], (D_MODEL, 1, D_CONV), jnp.float32) * 0.3
        conv_b = jax.random.normal(ks[2], (D_MODEL,), jnp.float32) * 0.1
        x_proj_dt_w = jax.random.normal(ks[3], (DT_RANK, D_MODEL), jnp.float32) * D_MODEL ** (-0.5)
        s = DT_RANK ** (-0.5)
        dt_proj_w = jax.random.uniform(ks[4], (D_MODEL, DT_RANK), jnp.float32, -s, s)
        dt = jnp.exp(jax.random.uniform(ks[5], (D_MODEL,), jnp.float32) * (np.log(0.1) - np.log(0.001)) + np.log(0.001))
        dt_proj_b = dt + jnp.log(-jnp.expm1(-dt))
        B_proj_w = jax.random.normal(ks[6], (D_STATE, D_MODEL), jnp.float32) * D_MODEL ** (-0.5)
        C_proj_w = jax.random.normal(ks[7], (D_STATE, D_MODEL), jnp.float32) * D_MODEL ** (-0.5)
        A_log = jnp.log(jnp.tile(jnp.arange(1, D_STATE + 1, dtype=jnp.float32), (D_MODEL, 1)))
        D_param = jnp.ones((D_MODEL,), jnp.float32)
        return dict(x=x, conv_w=conv_w, conv_b=conv_b, x_proj_dt_w=x_proj_dt_w, dt_proj_w=dt_proj_w, dt_proj_b=dt_proj_b, B_proj_w=B_proj_w, C_proj_w=C_proj_w, A_log=A_log, D_param=D_param)
    _L0_attn_b_in = _L0_attn_b_setup()

    def _L0_ffn_setup():
        import jax, jax.numpy as jnp
        import numpy as np
        B, S, H, F, E, K = (2, 256, 256, 512, 8, 2)
        key = jax.random.key(seed)
        ks = jax.random.split(key, 5)
        scale_h = 1.0 / np.sqrt(H)
        scale_f = 1.0 / np.sqrt(F)
        return {'inputs': jax.random.normal(ks[0], (B, S, H), dtype=jnp.float32), 'router_w': jax.random.normal(ks[1], (H, E), dtype=jnp.float32) * scale_h, 'w1': jax.random.normal(ks[2], (E, H, F), dtype=jnp.float32) * scale_h, 'w3': jax.random.normal(ks[3], (E, H, F), dtype=jnp.float32) * scale_h, 'w2': jax.random.normal(ks[4], (E, F, H), dtype=jnp.float32) * scale_f}
    _L0_ffn_in = _L0_ffn_setup()
    _d = {'L0_attn_a_hidden_states': _L0_attn_a_in['hidden_states'], 'L0_attn_a_Wq': _L0_attn_a_in['Wq'], 'L0_attn_a_bq': _L0_attn_a_in['bq'], 'L0_attn_a_Wk': _L0_attn_a_in['Wk'], 'L0_attn_a_bk': _L0_attn_a_in['bk'], 'L0_attn_a_Wv': _L0_attn_a_in['Wv'], 'L0_attn_a_bv': _L0_attn_a_in['bv'], 'L0_attn_a_Wo': _L0_attn_a_in['Wo'], 'L0_attn_a_bo': _L0_attn_a_in['bo'], 'L0_attn_b_conv_w': _L0_attn_b_in['conv_w'], 'L0_attn_b_conv_b': _L0_attn_b_in['conv_b'], 'L0_attn_b_x_proj_dt_w': _L0_attn_b_in['x_proj_dt_w'], 'L0_attn_b_dt_proj_w': _L0_attn_b_in['dt_proj_w'], 'L0_attn_b_dt_proj_b': _L0_attn_b_in['dt_proj_b'], 'L0_attn_b_B_proj_w': _L0_attn_b_in['B_proj_w'], 'L0_attn_b_C_proj_w': _L0_attn_b_in['C_proj_w'], 'L0_attn_b_A_log': _L0_attn_b_in['A_log'], 'L0_attn_b_D_param': _L0_attn_b_in['D_param'], 'L0_ffn_router_w': _L0_ffn_in['router_w'], 'L0_ffn_w1': _L0_ffn_in['w1'], 'L0_ffn_w3': _L0_ffn_in['w3'], 'L0_ffn_w2': _L0_ffn_in['w2']}
    _x0 = _d['L0_attn_a_hidden_states']
    _d['L0_attn_a_hidden_states'] = jax.random.normal(jax.random.fold_in(jax.random.key(seed), 1), (8, 512, 256), dtype=_x0.dtype)
    del _x0
    return _d

def reference(L0_attn_a_hidden_states, L0_attn_a_Wq, L0_attn_a_bq, L0_attn_a_Wk, L0_attn_a_bk, L0_attn_a_Wv, L0_attn_a_bv, L0_attn_a_Wo, L0_attn_a_bo, L0_attn_b_conv_w, L0_attn_b_conv_b, L0_attn_b_x_proj_dt_w, L0_attn_b_dt_proj_w, L0_attn_b_dt_proj_b, L0_attn_b_B_proj_w, L0_attn_b_C_proj_w, L0_attn_b_A_log, L0_attn_b_D_param, L0_ffn_router_w, L0_ffn_w1, L0_ffn_w3, L0_ffn_w2):

    def _L0_attn_a_ref(hidden_states, Wq, bq, Wk, bk, Wv, bv, Wo, bo):
        import jax, jax.numpy as jnp
        import numpy as np
        B, S, H, NH = (2, 512, 256, 16)
        HD = H // NH
        b, s, h = hidden_states.shape
        nh, hd = (NH, h // NH)

        def proj(W, bias):
            y = hidden_states @ W.T + bias
            return y.reshape(b, s, nh, hd).transpose(0, 2, 1, 3)
        q = proj(Wq, bq)
        k = proj(Wk, bk)
        v = proj(Wv, bv)
        scale = jnp.sqrt(jnp.asarray(hd, dtype=q.dtype))
        scores = jnp.einsum('bhqd,bhkd->bhqk', q, k) / scale
        pos = jnp.arange(s)
        causal = pos[:, None] < pos[None, :]
        scores = jnp.where(causal[None, None], -jnp.inf, scores)
        attn = jax.nn.softmax(scores, axis=-1)
        out = jnp.einsum('bhqk,bhkd->bhqd', attn, v)
        out = out.transpose(0, 2, 1, 3).reshape(b, s, h)
        return out @ Wo.T + bo

    def _L0_attn_b_ref(x, conv_w, conv_b, x_proj_dt_w, dt_proj_w, dt_proj_b, B_proj_w, C_proj_w, A_log, D_param):
        import jax, jax.numpy as jnp
        import numpy as np
        BATCH, SEQ, D_MODEL = (2, 512, 256)
        D_STATE, D_CONV = (16, 4)
        DT_RANK = 64

        def _forward(x, conv_w, conv_b, x_proj_dt_w, dt_proj_w, dt_proj_b, B_proj_w, C_proj_w, A_log, D_param):
            B, L, D = x.shape
            xc = jax.lax.conv_general_dilated(x.transpose(0, 2, 1), conv_w, window_strides=(1,), padding=[(D_CONV - 1, 0)], feature_group_count=D, dimension_numbers=('NCH', 'OIH', 'NCH'))
            xc = jax.nn.silu((xc + conv_b[None, :, None]).transpose(0, 2, 1))
            dt = jax.nn.softplus(xc @ x_proj_dt_w.T @ dt_proj_w.T + dt_proj_b)
            B_ssm = xc @ B_proj_w.T
            C_ssm = xc @ C_proj_w.T
            A = -jnp.exp(A_log)
            dA = jnp.exp(dt[..., None] * A)
            dBx = dt[..., None] * B_ssm[:, :, None, :] * xc[..., None]

            def step(h, inp):
                dA_t, dBx_t, C_t = inp
                h = dA_t * h + dBx_t
                y_t = jnp.einsum('bdn,bn->bd', h, C_t)
                return (h, y_t)
            h0 = jnp.zeros((B, D, D_STATE), x.dtype)
            _, ys = jax.lax.scan(step, h0, (dA.transpose(1, 0, 2, 3), dBx.transpose(1, 0, 2, 3), C_ssm.transpose(1, 0, 2)))
            return ys.transpose(1, 0, 2) + D_param * xc
        return _forward(x, conv_w, conv_b, x_proj_dt_w, dt_proj_w, dt_proj_b, B_proj_w, C_proj_w, A_log, D_param)

    def _L0_ffn_ref(inputs, router_w, w1, w3, w2):
        import jax, jax.numpy as jnp
        import numpy as np
        B, S, H, F, E, K = (2, 256, 256, 512, 8, 2)
        b, s, h = inputs.shape
        x = inputs.reshape(-1, h)
        logits = x @ router_w
        top_vals, top_idx = jax.lax.top_k(logits, K)
        importance = jax.nn.softmax(top_vals.astype(jnp.float32), axis=-1).astype(x.dtype)
        one_hot = top_idx[..., None] == jnp.arange(E)[None, None, :]
        combine = jnp.sum(jnp.where(one_hot, importance[..., None], 0.0), axis=1)
        gate = jax.nn.silu(jnp.einsum('th,ehf->etf', x, w1))
        up = jnp.einsum('th,ehf->etf', x, w3)
        expert_out = jnp.einsum('etf,efh->eth', gate * up, w2)
        out = jnp.einsum('te,eth->th', combine, expert_out)
        return out.reshape(b, s, h)
    x = L0_attn_a_hidden_states
    x = x + _L0_attn_a_ref(_layernorm(x, axis=-1), L0_attn_a_Wq, L0_attn_a_bq, L0_attn_a_Wk, L0_attn_a_bk, L0_attn_a_Wv, L0_attn_a_bv, L0_attn_a_Wo, L0_attn_a_bo)
    x = x + _L0_ffn_ref(_layernorm(x, axis=-1), L0_ffn_router_w, L0_ffn_w1, L0_ffn_w3, L0_ffn_w2)
    x = x + _L0_attn_b_ref(_layernorm(x, axis=-1), L0_attn_b_conv_w, L0_attn_b_conv_b, L0_attn_b_x_proj_dt_w, L0_attn_b_dt_proj_w, L0_attn_b_dt_proj_b, L0_attn_b_B_proj_w, L0_attn_b_C_proj_w, L0_attn_b_A_log, L0_attn_b_D_param)
    x = x + _L0_ffn_ref(_layernorm(x, axis=-1), L0_ffn_router_w, L0_ffn_w1, L0_ffn_w3, L0_ffn_w2)
    return x

_drawn_inputs = setup_inputs


def setup_inputs(seed=0):
    import zlib

    import numpy as np

    out = dict(_drawn_inputs(seed))
    spreads = {'L0_attn_b_D_param': (1.0, 0.2)}
    factors = {'L0_attn_a_Wq': 3.268,
     'L0_attn_a_bq': 8.0,
     'L0_attn_a_Wk': 3.382,
     'L0_attn_a_bk': 8.0,
     'L0_attn_b_x_proj_dt_w': 5.542,
     'L0_attn_b_dt_proj_w': 5.835,
     'L0_attn_b_dt_proj_b': 3.507,
     'L0_attn_b_A_log': 3.353}
    for name, (base, spread) in spreads.items():
        noise = np.random.default_rng([zlib.crc32(name.encode()), seed]).standard_normal(out[name].shape)
        drawn = base * np.exp(spread * noise) if base else spread * noise
        out[name] = jnp.asarray(drawn.astype(out[name].dtype))
    for name, factor in factors.items():
        out[name] = (out[name] * factor).astype(out[name].dtype)
    return out
```

```python
from contextlib import ExitStack

import concourse.bass as bass
from concourse import mybir

F32 = mybir.dt.float32
BF16 = mybir.dt.bfloat16
I32 = mybir.dt.int32
ALU = mybir.AluOpType
ACT = mybir.ActivationFunctionType
AX = mybir.AxisListType

P = 128
B, S, H = 8, 512, 256
NH, HD = 16, 16
T = B * S
NT = T // P
QT = S // P
HC = H // P
E, F = 8, 512
FC = F // P
EPS = 1e-5
SPLITS = 3
PAIRS = ((0, 0), (0, 1), (1, 0), (1, 1), (0, 2), (2, 0))
KROWS = len(PAIRS) * HD
MROWS = KROWS + SPLITS
ROUTED = 2 * T
MTILES = ROUTED // P + E - 1
MTILES += MTILES % 2
LB = 4
RB = 4
NS, RANK, TAPS = 16, 64, 4
BCR = 2 * NS
MASKED = -1e30
BIG = 3.0e38
LN_EXP = 'natural_log_exp_and_others'
MAGIC = 12582912.0

CF_ID, CF_TRI, CF_ONE, CF_IOTA, CF_SCAN, CF_TB = 0, 128, 256, 384, 384 + NT * E, 384 + 2 * NT * E
CF_N = CF_TB + MTILES * E
CB_ID, CB_MT, CB_MR, CB_SEL = 0, 128, 256, 384
CB_N = CB_SEL + BCR * P


def rows(v, n):
    return v.rearrange("(a n) -> a n", a=1).to_broadcast([P, n])


def build_attention(nc, sems, x, cf, cb, d, eps):
    ident = cf[:, CF_ID:CF_ID + P]
    ident_b = cb[:, CB_ID:CB_ID + P]
    mask_t = cb[:, CB_MT:CB_MT + P]
    mask_r = cb[:, CB_MR:CB_MR + P]
    KOFF = [0, 512, 896, 1152]
    PTW = 1280
    HG = 32
    with ExitStack() as ctx:
        def sb(name, shape, dt=F32):
            return ctx.enter_context(nc.sbuf_tensor(name, shape, dt))

        def ps(name, shape):
            return ctx.enter_context(nc.psum_tensor(name, shape, F32))

        used = []

        def sem(name):
            used.append(sems.enter_context(nc.semaphore(name)))
            return used[-1]

        wqkvo = sb("wqkvo", [P, 4, HC, H])
        qkbias = sb("qkbias", [P, 4])
        vbias = sb("vbias", [P, H])
        obias = sb("obias", [P, H])
        stats = sb("at_stats", [P, QT, 6])
        mv = sb("at_mv", [P, QT, 2])
        lnvar = sb("at_lnvar", [P, QT])
        rstd = sb("at_rstd", [P, QT])
        pause = sb("at_pause", [P, 1])
        xh = sb("at_xh", [P, QT, H])
        xT = sb("at_xT", [P, HC, S])
        qk32 = sb("qk32", [P, 4, S])
        parts = sb("parts", [P, SPLITS, 4, S], BF16)
        KS = [sb(f"KS{i}", [MROWS, NH, S], BF16) for i in range(2)]
        QS = [sb(f"QS{i}", [MROWS, NH, S], BF16) for i in range(2)]
        V = [sb(f"V{i}", [P, QT, NH, HG]) for i in range(2)]
        rowmax = sb("rowmax", [P, QT, NH])
        m32 = sb("m32", [NH, S])
        mparts = sb("mparts", [NH, SPLITS, S], BF16)
        probs = [sb(f"probs{i}", [P, PTW]) for i in range(2)]
        recip = sb("recip", [P, 2, QT, 4])
        oT = sb("oT", [P, S])
        attn = sb("attn", [P, QT, H])
        attnT = sb("attnT", [P, HC, S])
        scr = nc.dram_tensor("qk_parts", [2, SPLITS, 4, P, S], BF16).ap()

        sc = [ps(f"sc{i}", [P, 512]) for i in range(3)]
        mx = [ps(f"mx{i}", [P, 512]) for i in range(2)]
        O = ps("O", [P, 512])
        misc = [ps(f"misc{i}", [P, 512]) for i in range(2)]

        w_in = sem("w_in")
        ones_set = sem("ones_set")
        stat_done = sem("stat_done")
        var_ready = sem("var_ready")
        ln_done = sem("ln_done")
        rstd_ready = sem("rstd_ready")
        xh_ready = sem("xh_ready")
        xT_psum = sem("xT_psum")
        xT_ready = sem("xT_ready")
        qk_psum = sem("qk_psum")
        qk_evac = sem("qk_evac")
        qk_rest1 = sem("qk_rest1")
        qk_part2 = sem("qk_part2")
        qk_part3 = sem("qk_part3")
        parts_out = sem("parts_out")
        stacked = sem("stacked")
        v_psum = sem("v_psum")
        v_evac = sem("v_evac")
        mx_psum = sem("mx_psum")
        mx_read = sem("mx_read")
        mT_psum = sem("mT_psum")
        mT_evac = sem("mT_evac")
        m_rest1 = sem("m_rest1")
        m_part2 = sem("m_part2")
        m_part3 = sem("m_part3")
        m_stacked = sem("m_stacked")
        sc_psum = sem("sc_psum")
        exp_done = sem("exp_done")
        pv_done = sem("pv_done")
        oT_evac = sem("oT_evac")
        o_turned = sem("o_turned")
        recip_done = sem("recip_done")
        o_read = sem("o_read")
        aT_psum = sem("aT_psum")
        aT_evac = sem("aT_evac")
        wo_psum = sem("wo_psum")
        wo_sum = sem("wo_sum")
        wo_evac = sem("wo_evac")
        NW = 7

        def schedule(eng, norm, project, values, maxima, attend):
            for b in range(2):
                norm(b)
                project(b, b)
                values(b, b)
                if b == 0:
                    maxima(0, 0)
            attend(0, 0, True, True)
            with eng.Fori(0, (B - 4) // 2) as it:
                for par in range(2):
                    attend(2 * it + 1 + par, 1 - par, True, True)
            attend(B - 3, 1, True, True)
            attend(B - 2, 0, True, False)
            attend(B - 1, 1, False, False)

        SPLIT_SLOTS = (6, 8, 10)
        NORM_SLOT, XT_SLOT, Q_SLOT, K_SLOT = 0, 2, 3, 4
        units = [(h, i) for h in range(NH) for i in range(QT)]
        FIRST_SLOT, PER_SLOT = 5, 6

        def unit_range(slot):
            if slot < FIRST_SLOT:
                return range(0)
            a = (slot - FIRST_SLOT) * PER_SLOT
            return range(a, min(a + PER_SLOT, len(units)))

        block = ctx.enter_context(nc.Block())

        @block.sync
        def _(sp):
            for i, w in enumerate(("Wq", "Wk", "Wv", "Wo")):
                sp.dma_start(wqkvo[:, i], d[w].rearrange("(c p) n -> p c n", p=P)).then_inc(w_in, 16)
            sp.dma_start(qkbias[:, :], d["bqk"]).then_inc(w_in, 16)
            sp.dma_start(vbias[:, :], rows(d["bv"], H)).then_inc(w_in, 16)
            sp.dma_start(obias[:, :], rows(d["bo"], H)).then_inc(w_in, 16)

            def store_parts(b, par):
                split, read = b + 1, 16 * 12 * (b - 1)
                sp.compute_val(read)
                sp.wait_ge(qk_part3, split)
                if not isinstance(b, int) or b >= 2:
                    sp.wait_ge(stacked, read)
                sp.dma_start(scr[par].rearrange("s j p t -> p s j t"), parts[:, :, :, :]).then_inc(parts_out, 16)

            def stack(b, par):
                written, used = 16 * (b + 1), NH * (b - 1)
                sp.compute_val(used)
                sp.wait_ge(parts_out, written)
                if not isinstance(b, int) or b >= 2:
                    sp.wait_ge(pv_done, used)
                for n, (kp, qp) in enumerate(PAIRS):
                    r = slice(HD * n, HD * n + HD)
                    sp.dma_start(QS[par][r], scr[par, qp, 0:2].rearrange("m (g e) t -> e (m g) t", e=HD)).then_inc(stacked, 16)
                    sp.dma_start(KS[par][r], scr[par, kp, 2:4].rearrange("m (g e) t -> e (m g) t", e=HD)).then_inc(stacked, 16)

            def maxima(b, par):
                sp.wait_ge(m_part3, b + 1)
                for s in range(SPLITS):
                    sp.dma_start(QS[par][KROWS + s:KROWS + s + 1], mparts[:, s, :]).then_inc(m_stacked, 16)

            def norm(b):
                pass

            def project(b, par):
                store_parts(b, par)
                stack(b, par)

            def values(b, par):
                pass

            def attend(b, par, nxt, more):
                if more:
                    store_parts(b + 2, par)
                if nxt:
                    maxima(b + 1, 1 - par)
                if more:
                    stack(b + 2, par)

            schedule(sp, norm, project, values, maxima, attend)

        @block.gpsimd
        def _(pool):
            def norm(b):
                pass

            def project(b, par):
                pass

            def values(b, par):
                pass

            def maxima(b, par):
                pool.wait_ge(mT_evac, b + 1)
                nc.gpsimd.tensor_tensor(m32[:, :], m32[:, :], mparts[:, 0, :], ALU.subtract).then_inc(m_rest1, 1)
                pool.wait_ge(m_part2, b + 1)
                nc.gpsimd.tensor_tensor(mparts[:, 2, :], m32[:, :], mparts[:, 1, :], ALU.subtract).then_inc(m_part3, 1)

            def attend(b, par, nxt, more):
                if nxt:
                    maxima(b + 1, 1 - par)

            schedule(pool, norm, project, values, maxima, attend)

        @block.scalar
        def _(act):
            def norm(b):
                act.wait_ge(var_ready, b + 1)
                nc.scalar.activation(lnvar[:, :], mv[:, :, 1], ACT.Ln, bias=eps[:, 0:1]).then_inc(ln_done, 1)
                act.wait_ge(ln_done, b + 1)
                nc.scalar.activation(rstd[:, :], lnvar[:, :], ACT.Exp, scale=-0.5).then_inc(rstd_ready, 1)

            def turned(b):
                for c in range(HC):
                    act.wait_ge(xT_psum, HC * b + c + 1)
                    nc.scalar.copy(xT[:, c, :], misc[1 - c][:, :]).then_inc(xT_ready, 1)

            def queries_keys(b, js):
                if not isinstance(b, int) or b >= 1:
                    act.wait_ge(qk_part3, b)
                    act.wait_ge(parts_out, 16 * b)
                for j in js:
                    act.wait_ge(qk_psum, 4 * b + j + 1)
                    nc.scalar.activation(parts[:, 0, j, :], misc[1 - j % 2][:, :], ACT.Identity, bias=qkbias[:, j:j + 1])
                    nc.scalar.activation(qk32[:, j, :], misc[1 - j % 2][:, :], ACT.Identity, bias=qkbias[:, j:j + 1]).then_inc(qk_evac, 1)

            def project(b, par):
                turned(b)
                queries_keys(b, range(4))

            def values(b, par):
                pass

            def maxima(b, par):
                act.wait_ge(mT_psum, b + 1)
                if not isinstance(b, int) or b >= 1:
                    act.wait_ge(m_stacked, 16 * SPLITS * b)
                nc.scalar.mul(mparts[:, 0, :], misc[0][0:NH, :], -1.0)
                nc.scalar.mul(m32[:, :], misc[0][0:NH, :], -1.0).then_inc(mT_evac, 1)
                act.wait_ge(m_rest1, b + 1)
                nc.scalar.copy(mparts[:, 1, :], m32[:, :]).then_inc(m_part2, 1)

            def group_out(b, g):
                act.wait_ge(pv_done, NH * b + 4 * g + 4)
                if g or not isinstance(b, int) or b >= 1:
                    act.wait_ge(o_turned, NH // 4 * b + g)
                nc.scalar.copy(oT[:, :], O[:, :]).then_inc(oT_evac, 1)

            def attend(b, par, nxt, more):
                for h in range(NH):
                    if h >= 2:
                        act.wait_ge(pv_done, NH * b + h - 1)
                    elif not isinstance(b, int) or b >= 1:
                        act.wait_ge(pv_done, NH * b + h - 1)
                    for n, (c0, c1) in enumerate(((0, 512), (512, 896), (896, 1280))):
                        act.wait_ge(sc_psum, 3 * (NH * b + h) + n + 1)
                        nc.scalar.activation(probs[h % 2][:, c0:c1], sc[n][:, 0:c1 - c0], ACT.Exp,
                                             scale=HD ** -0.5).then_inc(exp_done, 1)
                    if h % 4 == 0 and h:
                        group_out(b, h // 4 - 1)
                    if more and h == NORM_SLOT:
                        norm(b + 2)
                    if more and h == XT_SLOT:
                        turned(b + 2)
                    if more and h == Q_SLOT:
                        queries_keys(b + 2, range(2))
                    if more and h == K_SLOT:
                        queries_keys(b + 2, range(2, 4))
                group_out(b, NH // 4 - 1)
                if nxt:
                    maxima(b + 1, 1 - par)
                for c in range(HC):
                    act.wait_ge(aT_psum, HC * b + c + 1)
                    nc.scalar.copy(attnT[:, c, :], misc[1 - c][:, :]).then_inc(aT_evac, 1)

            nc.scalar.preload_act_table_set(LN_EXP)
            act.wait_ge(w_in, 16 * NW)
            schedule(act, norm, project, values, maxima, attend)

        @block.vector
        def _(dve):
            def norm_stats(b):
                for i in range(QT):
                    last = nc.vector.bn_stats(stats[:, i, :], x[:, QT * b + i, :])
                last.then_inc(stat_done, 1)
                dve.wait_ge(stat_done, b + 1)
                nc.vector.memset(pause[:, :], 0.0)
                for i in range(QT):
                    last = nc.vector.bn_aggr(mv[:, i, :], stats[:, i, :])
                last.then_inc(var_ready, 1)

            def normalize(b):
                dve.wait_ge(rstd_ready, b + 1)
                if not isinstance(b, int) or b >= 1:
                    dve.wait_ge(xT_psum, HC * b)
                for i in range(QT):
                    last = nc.vector.tensor_scalar(xh[:, i, :], x[:, QT * b + i, :], mv[:, i, 0:1], rstd[:, i:i + 1],
                                                   ALU.subtract, ALU.mult)
                last.then_inc(xh_ready, 1)

            def values(b, par):
                if not isinstance(b, int) or b >= 2:
                    dve.wait_ge(pv_done, NH * (b - 1))
                for n in range(2):
                    dve.wait_ge(v_psum, 2 * b + n + 1)
                    nc.vector.tensor_tensor(
                        V[par][:, 2 * n:2 * n + 2, :, 0:HD],
                        misc[1 - n][:, :].rearrange("p (i h e) -> p i h e", i=2, h=NH),
                        vbias[:, :].rearrange("p (a h e) -> p a h e", a=1, h=NH).to_broadcast([P, 2, NH, HD]),
                        ALU.add).then_inc(v_evac, 1)

            def unit(b, u):
                h, i = units[u]
                dve.wait_ge(mx_psum, len(units) * b + u + 1)
                nc.vector.tensor_reduce(rowmax[:, i, h:h + 1], mx[u % 2][:, 0:(i + 1) * P], AX.X, ALU.max).then_inc(mx_read, 1)

            def split(b, step):
                if step == 0:
                    dve.wait_ge(qk_evac, 4 * (b + 1))
                    nc.vector.tensor_tensor(qk32[:, :, :], qk32[:, :, :], parts[:, 0, :, :], ALU.subtract).then_inc(qk_rest1, 1)
                elif step == 1:
                    dve.wait_ge(qk_rest1, b + 1)
                    nc.vector.tensor_copy(parts[:, 1, :, :], qk32[:, :, :]).then_inc(qk_part2, 1)
                else:
                    dve.wait_ge(qk_part2, b + 1)
                    nc.vector.tensor_tensor(parts[:, 2, :, :], qk32[:, :, :], parts[:, 1, :, :], ALU.subtract).then_inc(qk_part3, 1)

            def norm(b):
                norm_stats(b)
                normalize(b)

            def project(b, par):
                for step in range(3):
                    split(b, step)

            def maxima(b, par):
                for u in range(len(units)):
                    unit(b, u)

            def group(b, g):
                o = misc[g % 2][:, :].rearrange("p (i h e) -> p i h e", i=QT, h=4)
                dve.wait_ge(o_turned, NH // 4 * b + g + 1)
                if g == 0 and (not isinstance(b, int) or b >= 1):
                    dve.wait_ge(aT_psum, HC * b)
                nc.vector.reciprocal(recip[:, g % 2], o[:, :, :, HD]).then_inc(recip_done, 1)
                dve.wait_ge(recip_done, NH // 4 * b + g + 1)
                a = attn[:, :, 64 * g:64 * g + 64].rearrange("p i (h e) -> p i h e", h=4)
                nc.vector.tensor_tensor(a, o[:, :, :, 0:HD],
                                        recip[:, g % 2].rearrange("p i (h a) -> p i h a", a=1).to_broadcast([P, QT, 4, HD]),
                                        ALU.mult).then_inc(o_read, 1)

            def attend(b, par, nxt, more):
                for h in range(NH):
                    if nxt:
                        for u in unit_range(h):
                            unit(b + 1, u)
                    if h % 4 == 1 and h > 1:
                        group(b, h // 4 - 1)
                    if more and h == NORM_SLOT:
                        norm(b + 2)
                    if more and h in SPLIT_SLOTS:
                        split(b + 2, SPLIT_SLOTS.index(h))
                group(b, NH // 4 - 1)
                for n in range(2):
                    dve.wait_ge(wo_psum, 2 * b + n + 1)
                    xb = x[:, bass.ds(QT * b + 2 * n, 2), :]
                    pair = misc[1 - n][:, :].rearrange("p (i e) -> p i e", i=2)
                    nc.vector.tensor_tensor(xb, xb, pair, ALU.add).then_inc(wo_evac, 1)
                    dve.wait_ge(wo_evac, 2 * b + n + 1)
                    nc.vector.tensor_tensor(
                        xb, xb, obias[:, :].rearrange("p (a e) -> p a e", a=1).to_broadcast([P, 2, H]),
                        ALU.add).then_inc(wo_sum, 1)
                if more:
                    values(b + 2, par)

            for i in range(2):
                nc.vector.memset(KS[i][KROWS:MROWS], 1.0).then_inc(ones_set, 1)
                nc.vector.memset(V[i][:, :, :, HD:HG], 0.0).then_inc(ones_set, 1)
                dve.wait_ge(ones_set, 3 * i + 2)
                nc.vector.memset(V[i][:, :, :, HD:HD + 1], 1.0).then_inc(ones_set, 1)
            dve.wait_ge(w_in, 16 * NW)
            schedule(dve, norm, project, values, maxima, attend)
            dve.wait_ge(wo_sum, 2 * B)

        @block.tensor
        def _(pe):
            def turn_tokens(b):
                pe.wait_ge(xh_ready, b + 1)
                if not isinstance(b, int) or b >= 1:
                    pe.wait_ge(v_evac, 2 * b)
                if isinstance(b, int) and b == 1:
                    pe.wait_ge(mT_evac, b)
                for c in range(HC):
                    for i in range(QT):
                        last = nc.tensor.transpose(misc[1 - c][:, i * P:(i + 1) * P], xh[:, i, c * P:(c + 1) * P], ident)
                    last.then_inc(xT_psum, 1)

            def queries_keys(b, js):
                for j in js:
                    if j < 2:
                        pe.wait_ge(xT_ready, HC * b + 2)
                    else:
                        pe.wait_ge(qk_evac, 4 * b + j - 1)
                    for c in range(HC):
                        last = nc.tensor.matmul(misc[1 - j % 2][:, :], wqkvo[:, j // 2, c, (j % 2) * P:(j % 2 + 1) * P],
                                                xT[:, c, :], start=c == 0, stop=c == HC - 1)
                    last.then_inc(qk_psum, 1)

            def norm(b):
                pass

            def project(b, par):
                turn_tokens(b)
                queries_keys(b, range(4))

            def values(b, par):
                for n in range(2):
                    if isinstance(b, int) and b < 2:
                        pe.wait_ge(qk_evac, 4 * b + n + 3)
                    else:
                        pe.wait_ge(wo_evac, 2 * (b - 2) + n + 1)
                    for i in range(2):
                        for c in range(HC):
                            t = 2 * n + i
                            last = nc.tensor.matmul(misc[1 - n][:, i * H:(i + 1) * H], xT[:, c, t * P:(t + 1) * P],
                                                    wqkvo[:, 2, c, :], start=c == 0, stop=c == HC - 1)
                    last.then_inc(v_psum, 1)

            def unit(b, par, u):
                h, i = units[u]
                if u >= 2 or not isinstance(b, int) or b >= 1:
                    pe.wait_ge(mx_read, len(units) * b + u - 1)
                w = (i + 1) * P
                nc.tensor.matmul(mx[u % 2][:, 0:w], QS[par][0:KROWS, h, i * P:w], KS[par][0:KROWS, h, 0:w], start=True, stop=False)
                nc.tensor.matmul(mx[u % 2][:, i * P:w], ident_b, mask_r, start=False, stop=True).then_inc(mx_psum, 1)

            def turn_maxima(b):
                pe.wait_ge(mx_read, len(units) * (b + 1))
                if isinstance(b, int) and b == 0:
                    pe.wait_ge(v_evac, 2)
                else:
                    pe.wait_ge(o_read, NH // 4 * b)
                for i in range(QT):
                    last = nc.tensor.transpose(misc[0][0:NH, i * P:(i + 1) * P], rowmax[:, i, :], ident)
                last.then_inc(mT_psum, 1)

            def maxima(b, par):
                pe.wait_ge(stacked, 16 * 12 * (b + 1))
                for u in range(len(units)):
                    unit(b, par, u)
                turn_maxima(b)

            def scores(b, par, h, ahead):
                for n, kts in enumerate(((0,), (1,), (2, 3))):
                    if n:
                        ahead(2)
                    if h >= 1 or not isinstance(b, int) or b >= 1:
                        pe.wait_ge(exp_done, 3 * (NH * b + h - 1) + n + 1)
                    at = 0
                    for kt in kts:
                        w = S - kt * P
                        nc.tensor.matmul(sc[n][:, at:at + w], KS[par][:, h, kt * P:(kt + 1) * P], QS[par][:, h, kt * P:S],
                                         start=True, stop=False)
                        last = nc.tensor.matmul(sc[n][:, at:at + P], ident_b, mask_t, start=False, stop=True)
                        at += w
                    last.then_inc(sc_psum, 1)

            def weigh(b, par, h, ahead):
                pe.wait_ge(exp_done, 3 * (NH * b + h + 1))
                if h % 4 == 0 and (h or not isinstance(b, int) or b >= 1):
                    pe.wait_ge(oT_evac, NH // 4 * b + h // 4)
                r = slice(HG * (h % 4), HG * (h % 4) + HG)
                for kt in range(QT):
                    if kt == 1:
                        ahead(1)
                    last = nc.tensor.matmul(O[r, kt * P:S], V[par][:, kt, h, :], probs[h % 2][:, KOFF[kt]:KOFF[kt] + S - kt * P],
                                            start=kt == 0, stop=kt == QT - 1, skip_group_check=True)
                last.then_inc(pv_done, 1)

            def turn_heads(b, g, nxt, more):
                pe.wait_ge(oT_evac, NH // 4 * b + g + 1)
                if g >= 2:
                    pe.wait_ge(o_read, NH // 4 * b + g - 1)
                elif more:
                    pe.wait_ge(qk_evac, 4 * (b + 2) + 4)
                elif nxt:
                    pe.wait_ge(v_evac, 2 * (b + 2))
                else:
                    pe.wait_ge(wo_evac, 2 * b)
                for i in range(QT):
                    last = nc.tensor.transpose(misc[g % 2][:, i * P:(i + 1) * P], oT[:, i * P:(i + 1) * P], ident)
                last.then_inc(o_turned, 1)

            def attend(b, par, nxt, more):
                pe.wait_ge(m_stacked, 16 * SPLITS * (b + 1))
                for h in range(NH):
                    if nxt and h == FIRST_SLOT:
                        pe.wait_ge(stacked, 16 * 12 * (b + 2))
                    todo = list(unit_range(h)) if nxt else []

                    def ahead(n):
                        for u in todo[:n]:
                            unit(b + 1, 1 - par, u)
                        del todo[:n]

                    scores(b, par, h, ahead)
                    ahead(2)
                    if h:
                        weigh(b, par, h - 1, ahead)
                    ahead(8)
                    if more and h == XT_SLOT:
                        turn_tokens(b + 2)
                    if more and h == Q_SLOT:
                        queries_keys(b + 2, range(2))
                    if more and h == K_SLOT:
                        queries_keys(b + 2, range(2, 4))
                    if h % 4 == 1 and h > 1:
                        turn_heads(b, h // 4 - 1, nxt, more)
                weigh(b, par, NH - 1, ahead)
                turn_heads(b, NH // 4 - 1, nxt, more)
                if nxt:
                    turn_maxima(b + 1)
                pe.wait_ge(o_read, NH // 4 * (b + 1))
                if nxt:
                    pe.wait_ge(mT_evac, b + 2)
                for c in range(HC):
                    for i in range(QT):
                        last = nc.tensor.transpose(misc[1 - c][:, i * P:(i + 1) * P], attn[:, i, c * P:(c + 1) * P], ident)
                    last.then_inc(aT_psum, 1)
                pe.wait_ge(aT_evac, HC * (b + 1))
                for n in range(2):
                    for i in range(2):
                        for c in range(HC):
                            t = 2 * n + i
                            last = nc.tensor.matmul(misc[1 - n][:, i * H:(i + 1) * H], attnT[:, c, t * P:(t + 1) * P],
                                                    wqkvo[:, 3, c, :], start=c == 0, stop=c == HC - 1)
                    last.then_inc(wo_psum, 1)
                if more:
                    values(b + 2, par)

            pe.wait_ge(w_in, 16 * NW)
            pe.wait_ge(ones_set, 6)
            schedule(pe, norm, project, values, maxima, attend)
    return used


def build_route(nc, sems, tag, x, xh, cf, eps, router, xs, slots, weights, tile_expert, scattered):
    ident = cf[:, CF_ID:CF_ID + P]
    earlier = cf[:, CF_TRI:CF_TRI + P]
    ones = cf[:, CF_ONE:CF_ONE + P]
    iota = cf[:, CF_IOTA:CF_IOTA + NT * E]
    fresh = cf[:, CF_SCAN:CF_SCAN + NT * E]
    tiles = cf[:, CF_TB:CF_TB + MTILES * E]
    G = 4
    NG = NT // G
    with ExitStack() as ctx:
        def sb(name, shape, dt=F32):
            return ctx.enter_context(nc.sbuf_tensor(f"{tag}_{name}", shape, dt))

        def ps(name, shape):
            return ctx.enter_context(nc.psum_tensor(f"{tag}_{name}", shape, F32))

        def sem(name):
            return sems.enter_context(nc.semaphore(f"{tag}_{name}"))

        stats = sb("stats", [P, 2, G, 6])
        mv = sb("mv", [P, 2, G, 2])
        lnvar = sb("lnvar", [P, G])
        rstd = sb("rstd", [P, 2, G])
        pause = sb("pause", [P, 1])
        xT = [sb(f"xT{i}", [P, G, HC, P]) for i in range(2)]
        lg = sb("lg", [P, NT, E])
        top = [sb(f"top{c}", [P, NT]) for c in range(2)]
        hot = [sb(f"hot{c}", [P, NT, E]) for c in range(2)]
        tmp = sb("tmp", [P, NT, E])
        pick = sb("pick", [P, NT])
        both = sb("both", [P, NT, E])
        total = sb("total", [P, E, NT])
        run = sb("run", [P, E, NT])
        padded = sb("padded", [P, E])
        ends = sb("ends", [P, E])
        starts = sb("starts", [P, E])
        place = sb("place", [P, NT, E])
        slotf = sb("slotf", [P, NT])
        gap = sb("gap", [P, NT])
        tcmp = sb("tcmp", [P, MTILES, E])
        tsum = sb("tsum", [P, MTILES])

        tp = [ps(f"tp{i}", [P, G, HC, P]) for i in range(2)]
        logits = ps("logits", [P, 512])
        ranks = ps("ranks", [P, 512])
        counts = ps("counts", [P, 512])

        stat_done = sem("stat_done")
        var_ready = sem("var_ready")
        ln_done = sem("ln_done")
        rstd_ready = sem("rstd_ready")
        xh_ready = sem("xh_ready")
        turned = sem("turned")
        xT_ready = sem("xT_ready")
        routed = sem("routed")
        step = sem("step")
        both_ready = sem("both_ready")
        counted = sem("counted")
        gap_ready = sem("gap_ready")
        ratio_ready = sem("ratio_ready")
        slot_ready = sem("slot_ready")

        block = ctx.enter_context(nc.Block())

        @block.scalar
        def _(act):
            nc.scalar.preload_act_table_set(LN_EXP)
            with act.Fori(0, NG // 2) as it:
                for par in range(2):
                    g = 2 * it + par
                    act.wait_ge(var_ready, g + 1)
                    nc.scalar.activation(lnvar[:, :], mv[:, par, :, 1], ACT.Ln, bias=eps[:, 0:1]).then_inc(ln_done, 1)
                    act.wait_ge(ln_done, g + 1)
                    nc.scalar.activation(rstd[:, par, :], lnvar[:, :], ACT.Exp, scale=-0.5).then_inc(rstd_ready, 1)
                    act.wait_ge(turned, g + 1)
                    nc.scalar.copy(xT[par][:, :, :, :], tp[par][:, :, :, :]).then_inc(xT_ready, 1)
            act.wait_ge(gap_ready, 1)
            nc.scalar.activation(gap[:, :], gap[:, :], ACT.Exp).then_inc(ratio_ready, 1)

        @block.tensor
        def _(pe):
            def logit(g):
                pe.wait_ge(xT_ready, g + 1)
                for i in range(G):
                    for c in range(HC):
                        last = nc.tensor.matmul(logits[:, (g * G + i) * E:(g * G + i + 1) * E], xT[g % 2][:, i, c, :],
                                                router[:, c, :], start=c == 0, stop=c == HC - 1)
                last.then_inc(routed, 1)

            for g in range(NG):
                pe.wait_ge(xh_ready, g + 1)
                if g >= 2:
                    pe.wait_ge(xT_ready, g - 1)
                for i in range(G):
                    for c in range(HC):
                        last = nc.tensor.transpose(tp[g % 2][:, i, c, :], xh[:, g * G + i, c * P:(c + 1) * P], ident)
                last.then_inc(turned, 1)
                if g:
                    logit(g - 1)
            logit(NG - 1)
            pe.wait_ge(both_ready, 1)
            b = both[:, :, :].rearrange("p t e -> p (t e)")
            nc.tensor.matmul(ranks[:, 0:NT * E], earlier, b, start=True, stop=True)
            nc.tensor.matmul(counts[:, 0:NT * E], ones, b, start=True, stop=True).then_inc(counted, 1)

        @block.vector
        def _(dve):
            done = [0]

            def then(ins):
                done[0] += 1
                ins.then_inc(step, 1)
                dve.wait_ge(step, done[0])

            def norm_stats(g, par):
                for i in range(G):
                    last = nc.vector.bn_stats(stats[:, par, i, :], x[:, G * g + i, :])
                last.then_inc(stat_done, 1)
                dve.wait_ge(stat_done, g + 1)
                nc.vector.memset(pause[:, :], 0.0)
                for i in range(G):
                    last = nc.vector.bn_aggr(mv[:, par, i, :], stats[:, par, i, :])
                last.then_inc(var_ready, 1)

            def normalize(g, par):
                dve.wait_ge(rstd_ready, g + 1)
                for i in range(G):
                    last = nc.vector.tensor_scalar(xh[:, G * g + i, :], x[:, G * g + i, :], mv[:, par, i, 0:1],
                                                   rstd[:, par, i:i + 1], ALU.subtract, ALU.mult)
                last.then_inc(xh_ready, 1)

            norm_stats(0, 0)
            with dve.Fori(0, NG // 2 - 1) as it:
                for par in range(2):
                    norm_stats(2 * it + par + 1, 1 - par)
                    normalize(2 * it + par, par)
            norm_stats(NG - 1, 1)
            normalize(NG - 2, 0)
            normalize(NG - 1, 1)

            def over_e(a, n=NT):
                return a.rearrange("p (t a) -> p t a", a=1).to_broadcast([P, n, E])

            io = iota.rearrange("p (t e) -> p t e", e=E)
            dve.wait_ge(routed, NG)
            then(nc.vector.tensor_copy(lg[:, :, :], logits[:, 0:NT * E].rearrange("p (t e) -> p t e", e=E)))
            for c in range(2):
                then(nc.vector.tensor_reduce(top[c][:, :], lg[:, :, :], AX.X, ALU.max))
                then(nc.vector.tensor_tensor(tmp[:, :, :], lg[:, :, :], over_e(top[c][:, :]), ALU.is_equal))
                then(nc.vector.tensor_tensor(tmp[:, :, :], tmp[:, :, :], io, ALU.mult))
                then(nc.vector.tensor_reduce(pick[:, :], tmp[:, :, :], AX.X, ALU.min))
                then(nc.vector.tensor_tensor(hot[c][:, :, :], io, over_e(pick[:, :]), ALU.is_equal))
                if c == 0:
                    then(nc.vector.scalar_tensor_tensor(out=lg[:, :, :], in0=hot[0][:, :, :], scalar=-BIG, in1=lg[:, :, :],
                                                        op0=ALU.mult, op1=ALU.add))
            nc.vector.tensor_tensor(both[:, :, :], hot[0][:, :, :], hot[1][:, :, :], ALU.add).then_inc(both_ready, 1)
            nc.vector.tensor_tensor(gap[:, :], top[1][:, :], top[0][:, :], ALU.subtract).then_inc(gap_ready, 1)
            dve.wait_ge(counted, 1)
            then(nc.vector.tensor_copy(total[:, :, :], counts[:, 0:NT * E].rearrange("p (t e) -> p e t", e=E)))
            flat = "p e t -> p (e t)"
            then(nc.vector.tensor_tensor_scan(run[:, :, :].rearrange(flat), fresh, total[:, :, :].rearrange(flat), 0.0,
                                              ALU.mult, ALU.add))
            then(nc.vector.tensor_scalar(padded[:, :], run[:, :, NT - 1], 1.0 / P, (P - 1) / (2.0 * P), ALU.mult, ALU.add))
            then(nc.vector.tensor_scalar(padded[:, :], padded[:, :], MAGIC, MAGIC, ALU.add, ALU.subtract))
            then(nc.vector.tensor_scalar(padded[:, :], padded[:, :], float(P), None, ALU.mult))
            then(nc.vector.tensor_tensor_scan(ends[:, :], ones[:, 0:E], padded[:, :], 0.0, ALU.mult, ALU.add))
            then(nc.vector.tensor_tensor(starts[:, :], ends[:, :], padded[:, :], ALU.subtract))
            then(nc.vector.tensor_tensor(run[:, :, :], run[:, :, :], total[:, :, :], ALU.subtract))
            then(nc.vector.tensor_tensor(run[:, :, :], run[:, :, :],
                                         starts[:, :].rearrange("p (e a) -> p e a", a=1).to_broadcast([P, E, NT]), ALU.add))
            then(nc.vector.tensor_tensor(place[:, :, :], ranks[:, 0:NT * E].rearrange("p (t e) -> p t e", e=E),
                                         run[:, :, :].rearrange("p e t -> p t e"), ALU.add))
            for c in range(2):
                then(nc.vector.tensor_tensor(tmp[:, :, :], hot[c][:, :, :], place[:, :, :], ALU.mult))
                then(nc.vector.tensor_reduce(slotf[:, :], tmp[:, :, :], AX.X, ALU.add))
                nc.vector.tensor_copy(slots[c][:, :], slotf[:, :]).then_inc(slot_ready, 1)
                dve.wait_ge(slot_ready, c + 1)
            tv = tiles.rearrange("p (t e) -> p t e", e=E)
            then(nc.vector.tensor_tensor(tcmp[:, :, :], tv, ends[:, :].rearrange("p (a e) -> p a e", a=1).to_broadcast([P, MTILES, E]),
                                         ALU.is_ge))
            then(nc.vector.tensor_reduce(tsum[:, :], tcmp[:, :, :], AX.X, ALU.add))
            then(nc.vector.tensor_scalar(tile_expert[:, :], tsum[:, :], float(E - 1), None, ALU.min))
            dve.wait_ge(ratio_ready, 1)
            then(nc.vector.tensor_scalar(slotf[:, :], gap[:, :], 1.0, None, ALU.add))
            then(nc.vector.reciprocal(weights[0][:, :], slotf[:, :]))
            then(nc.vector.tensor_tensor(weights[1][:, :], gap[:, :], weights[0][:, :], ALU.mult))

        @block.gpsimd
        def _(pool):
            for c in range(2):
                pool.wait_ge(slot_ready, c + 1)
                for t in range(NT):
                    pool.indirect_dma_start(out=xs, out_offset=bass.IndirectOffsetOnAxis(ap=slots[c][:, t:t + 1], axis=0),
                                            in_=xh[:, t, :], in_offset=None).then_inc(scattered, 16)
            pool.wait_ge(scattered, 16 * 2 * NT)


def build_experts(nc, sems, tag, cf, w1, w3, w2, w_count, xs, ys, tile_expert, stored):
    ident = cf[:, CF_ID:CF_ID + P]
    with ExitStack() as ctx:
        def sb(name, shape, dt=F32):
            return ctx.enter_context(nc.sbuf_tensor(f"{tag}_{name}", shape, dt))

        def ps(name, shape):
            return ctx.enter_context(nc.psum_tensor(f"{tag}_{name}", shape, F32))

        def sem(name):
            return sems.enter_context(nc.semaphore(f"{tag}_{name}"))

        xin = sb("xin", [P, LB, H])
        xT = [sb(f"exT{i}", [P, HC, P]) for i in range(2)]
        gate = [sb(f"gate{i}", [P, F]) for i in range(2)]
        hid = [sb(f"hid{i}", [P, F]) for i in range(2)]
        hT = [sb(f"hT{i}", [P, FC, P]) for i in range(2)]
        yo = sb("yo", [P, LB, H])
        xT_p = ps("xT_p", [P, 512])
        gate_p = [ps(f"gate_p{i}", [P, F]) for i in range(2)]
        up_p = [ps(f"up_p{i}", [P, F]) for i in range(2)]
        hT_p = ps("hT_p", [P, FC, P])
        out_p = [ps(f"out_p{i}", [P, 512]) for i in range(2)]

        loaded = [sem(f"loaded{i}") for i in range(LB)]
        x_turned = sem("ex_x_turned")
        xT_ready = sem("ex_xT_ready")
        gate_done = sem("ex_gate_done")
        up_done = sem("ex_up_done")
        silu_done = sem("ex_silu_done")
        hid_ready = sem("ex_hid_ready")
        h_turned = sem("ex_h_turned")
        hT_ready = sem("ex_hT_ready")
        out_done = sem("ex_out_done")
        y_ready = sem("ex_y_ready")

        xs_t = xs.rearrange("(t p) h -> t p h", p=P)
        ys_t = ys.rearrange("(t p) h -> t p h", p=P)
        block = ctx.enter_context(nc.Block())

        @block.sync
        def _(sp):
            for n in range(LB):
                sp.dma_start(xin[:, n, :], xs_t[n]).then_inc(loaded[n], 16)
            with sp.Fori(0, MTILES // LB - 1) as it:
                for n in range(LB):
                    tile, done = LB * it + n + LB, LB * it + n + 1
                    sp.wait_ge(x_turned, done)
                    sp.dma_start(xin[:, n, :], xs_t[tile]).then_inc(loaded[n], 16)

        @block.gpsimd
        def _(pool):
            with pool.Fori(0, MTILES // LB) as it:
                for n in range(LB):
                    pool.wait_ge(y_ready, LB * it + n + 1)
                    pool.dma_start(ys_t[LB * it + n], yo[:, n, :]).then_inc(stored[n], 16)
            for n in range(LB):
                pool.wait_ge(stored[n], 16 * (MTILES // LB))

        @block.scalar
        def _(act):
            nc.scalar.preload_act_table(ACT.Silu)

            def copy_x(t, par):
                act.wait_ge(x_turned, t + 1)
                nc.scalar.copy(xT[par][:, :, :], xT_p[:, 0:HC * P].rearrange("p (c t) -> p c t", c=HC)).then_inc(xT_ready, 1)

            def tile(t, par, more=True):
                act.wait_ge(gate_done, t + 1)
                nc.scalar.activation(gate[par][:, :], gate_p[par][:, :], ACT.Silu).then_inc(silu_done, 1)
                if more:
                    copy_x(t + 1, 1 - par)
                act.wait_ge(h_turned, t + 1)
                nc.scalar.copy(hT[par][:, :, :], hT_p[:, :, :]).then_inc(hT_ready, 1)

            copy_x(0, 0)
            with act.Fori(0, MTILES // 2 - 1) as it:
                for par in range(2):
                    tile(2 * it + par, par)
            tile(MTILES - 2, 0)
            tile(MTILES - 1, 1, more=False)

        @block.vector
        def _(dve):
            def put_out(it, t, par, n):
                dve.wait_ge(out_done, t + 1)
                nc.vector.tensor_copy(yo[:, n, :], out_p[par][:, 0:H]).then_inc(y_ready, 1)

            def gated(t, par):
                dve.wait_ge(up_done, t + 1)
                dve.wait_ge(silu_done, t + 1)
                nc.vector.tensor_tensor(hid[par][:, :], gate[par][:, :], up_p[par][:, :], ALU.mult).then_inc(hid_ready, 1)

            gated(0, 0)
            for n in range(1, LB):
                gated(n, n % 2)
                put_out(0, n - 1, (n - 1) % 2, n - 1)

            def round_(it):
                for n in range(LB):
                    gated(LB * it + n, n % 2)
                    m = (n - 1) % LB
                    if n:
                        dve.wait_ge(stored[m], 16 * it)
                    elif not isinstance(it, int):
                        dve.wait_ge(stored[m], 16 * (it - 1))
                    put_out(it, LB * it + n - 1, m % 2, m)

            round_(1)
            with dve.Fori(2, MTILES // LB) as it:
                round_(it)
            dve.wait_ge(stored[LB - 1], 16 * (MTILES // LB - 1))
            put_out(0, MTILES - 1, (MTILES - 1) % 2, LB - 1)

        @block.tensor
        def _(pe):
            def turn_x(t, par, n, round_):
                pe.wait_ge(loaded[n], 16 * (round_ + 1))
                if not isinstance(t, int) or t >= 1:
                    pe.wait_ge(xT_ready, t)
                for c in range(HC):
                    last = nc.tensor.transpose(xT_p[:, c * P:(c + 1) * P], xin[:, n, c * P:(c + 1) * P], ident)
                last.then_inc(x_turned, 1)

            def gate_up(t, par):
                e = nc.tensor.value_load(tile_expert[0:1, bass.ds(t, 1)], min_val=0, max_val=E - 1)
                pe.wait_ge(xT_ready, t + 1)
                if not isinstance(t, int) or t >= 2:
                    pe.wait_ge(silu_done, t - 1)
                for c in range(HC):
                    last = nc.tensor.matmul(gate_p[par][:, :], xT[par][:, c, :], w1[:, e, c, :], start=c == 0, stop=c == HC - 1)
                last.then_inc(gate_done, 1)
                if not isinstance(t, int) or t >= 2:
                    pe.wait_ge(hid_ready, t - 1)
                for c in range(HC):
                    last = nc.tensor.matmul(up_p[par][:, :], xT[par][:, c, :], w3[:, e, c, :], start=c == 0, stop=c == HC - 1)
                last.then_inc(up_done, 1)
                return e

            def turn_h(t, par):
                pe.wait_ge(hid_ready, t + 1)
                if not isinstance(t, int) or t >= 1:
                    pe.wait_ge(hT_ready, t)
                for c in range(FC):
                    last = nc.tensor.transpose(hT_p[:, c, :], hid[par][:, c * P:(c + 1) * P], ident)
                last.then_inc(h_turned, 1)

            def down(t, par):
                e = nc.tensor.value_load(tile_expert[0:1, bass.ds(t, 1)], min_val=0, max_val=E - 1)
                pe.wait_ge(hT_ready, t + 1)
                if not isinstance(t, int) or t >= 2:
                    pe.wait_ge(y_ready, t - 1)
                for c in range(FC):
                    last = nc.tensor.matmul(out_p[par][:, 0:H], hT[par][:, c, :], w2[:, e, c, :], start=c == 0, stop=c == FC - 1)
                last.then_inc(out_done, 1)

            for s, n in w_count:
                pe.wait_ge(s, n)
            turn_x(0, 0, 0, 0)
            gate_up(0, 0)
            turn_x(1, 1, 1, 0)

            def round_(it):
                for n in range(LB):
                    t = LB * it + n
                    turn_h(t, n % 2)
                    gate_up(t + 1, (n + 1) % 2)
                    turn_x(t + 2, n % 2, (n + 2) % LB, it + (n + 2) // LB)
                    down(t, n % 2)

            round_(0)
            with pe.Fori(1, MTILES // LB - 1) as it:
                round_(it)
            for t in range(MTILES - LB, MTILES):
                turn_h(t, t % 2)
                if t + 1 < MTILES:
                    gate_up(t + 1, (t + 1) % 2)
                if t + 2 < MTILES:
                    turn_x(t + 2, t % 2, (t + 2) % LB, (t + 2) // LB)
                down(t, t % 2)


def build_combine(nc, sems, tag, x, ys, slots, weights, fetched, out=None):
    with ExitStack() as ctx:
        got = ctx.enter_context(nc.sbuf_tensor(f"{tag}_got", [P, RB, 2, H], F32))
        first = sems.enter_context(nc.semaphore(f"{tag}_first"))
        added = sems.enter_context(nc.semaphore(f"{tag}_added"))
        written = sems.enter_context(nc.semaphore(f"{tag}_written"))
        block = ctx.enter_context(nc.Block())

        @block.gpsimd
        def _(pool):
            for t in range(NT):
                if t >= RB:
                    pool.wait_ge(added, t - RB + 1)
                for c in range(2):
                    pool.indirect_dma_start(out=got[:, t % RB, c, :], out_offset=None, in_=ys,
                                            in_offset=bass.IndirectOffsetOnAxis(ap=slots[c][:, t:t + 1], axis=0)
                                            ).then_inc(fetched[t % RB], 16)

        @block.vector
        def _(dve):
            with dve.Fori(0, NT // RB) as it:
                for n in range(RB):
                    t = RB * it + n
                    dve.wait_ge(fetched[n], 32 * (it + 1))
                    nc.vector.scalar_tensor_tensor(out=x[:, t, :], in0=got[:, n, 0, :], scalar=weights[0][:, bass.ds(t, 1)],
                                                   in1=x[:, t, :], op0=ALU.mult, op1=ALU.add).then_inc(first, 1)
                    dve.wait_ge(first, t + 1)
                    nc.vector.scalar_tensor_tensor(out=x[:, t, :], in0=got[:, n, 1, :], scalar=weights[1][:, bass.ds(t, 1)],
                                                   in1=x[:, t, :], op0=ALU.mult, op1=ALU.add).then_inc(added, 1)

        if out is not None:
            @block.sync
            def _(sp):
                with sp.Fori(0, NT // RB) as it:
                    first, done = RB * it, RB * it + RB
                    sp.wait_ge(added, done)
                    sp.dma_start(out[:, bass.ds(first, RB), :], x[:, bass.ds(first, RB), :]).then_inc(written, 16)
                sp.wait_ge(written, 16 * (NT // RB))


def build_mamba(nc, sems, x, cf, cb, d, eps):
    ident = cf[:, CF_ID:CF_ID + P]
    ones = cf[:, CF_ONE:CF_ONE + 1].rearrange("p (a t) -> p a t", a=1).to_broadcast([P, HC, S])
    with ExitStack() as ctx:
        def sb(name, shape, dt=F32):
            return ctx.enter_context(nc.sbuf_tensor(f"ma_{name}", shape, dt))

        def ps(name, shape):
            return ctx.enter_context(nc.psum_tensor(f"ma_{name}", shape, F32))

        def sem(name):
            return sems.enter_context(nc.semaphore(f"ma_{name}"))

        convw = sb("convw", [P, HC, TAPS])
        convb = sb("convb", [P, HC])
        wdt = sb("wdt", [P, HC, RANK])
        wdt2 = sb("wdt2", [RANK, H])
        dtb = sb("dtb", [P, HC])
        wbc = sb("wbc", [P, HC, SPLITS * BCR])
        A = sb("A", [P, HC, NS])
        D = sb("D", [P, HC])
        taps = sb("taps", [P, HC, TAPS, P])
        stats = sb("stats", [P, QT, 6])
        mv = sb("mv", [P, QT, 2])
        lnvar = sb("lnvar", [P, QT])
        rstd = sb("rstd", [P, QT])
        pause = sb("pause", [P, 1])
        xh = sb("xh", [P, QT, H])
        xp = sb("xp", [P, HC, TAPS - 1 + S])
        xc = [sb(f"xc{i}", [P, HC, S]) for i in range(2)]
        low = sb("low", [RANK, S])
        mag = sb("mag", [P, HC, S])
        ez = sb("ez", [P, HC, S])
        up = sb("up", [P, HC, S])
        pos = sb("pos", [P, HC, S])
        dt = [sb(f"dt{i}", [P, HC, S]) for i in range(2)]
        dtx = [sb(f"dtx{i}", [P, HC, S]) for i in range(2)]
        bc32 = sb("bc32", [SPLITS * BCR, S])
        bcs = [sb(f"bcs{i}", [SPLITS * BCR, S], BF16) for i in range(2)]
        dA = [sb(f"dA{i}", [P, HC, S]) for i in range(2)]
        dBx = [sb(f"dBx{i}", [P, HC, S]) for i in range(2)]
        hs = [sb(f"hs{i}", [P, HC, S]) for i in range(2)]
        hC = [sb(f"hC{i}", [P, HC, S]) for i in range(2)]
        yT = sb("yT", [P, HC, S])

        bB = [ps(f"bB{i}", [P, 512]) for i in range(2)]
        bC = [ps(f"bC{i}", [P, 512]) for i in range(2)]
        yp = ps("yp", [P, HC, 512])
        pp = [ps(f"pp{i}", [P, 512]) for i in range(2)]

        w_in = sem("w_in")
        setup = sem("setup")
        a_exp = sem("a_exp")
        stat_done = sem("stat_done")
        var_ready = sem("var_ready")
        ln_done = sem("ln_done")
        rstd_ready = sem("rstd_ready")
        xh_ready = sem("xh_ready")
        turned = sem("turned")
        xp_ready = sem("xp_ready")
        conv_done = sem("conv_done")
        xc_ready = sem("xc_ready")
        low_done = sem("low_done")
        low_ready = sem("low_ready")
        bc_done = sem("bc_done")
        bc_copied = sem("bc_copied")
        bc_rest1 = sem("bc_rest1")
        bc_part2 = sem("bc_part2")
        bc_ready = sem("bc_ready")
        z_done = sem("z_done")
        z_read = sem("z_read")
        exp_z = sem("exp_z")
        one_z = sem("one_z")
        soft_step = sem("soft_step")
        log_z = sem("log_z")
        dt_ready = sem("dt_ready")
        dtx_ready = sem("dtx_ready")
        spread_B = sem("spread_B")
        spread_C = sem("spread_C")
        dA_ready = sem("dA_ready")
        dBx_ready = sem("dBx_ready")
        scanned = sem("scanned")
        hC_ready = sem("hC_ready")
        summed = sem("summed")
        y_ready = sem("y_ready")
        y_turned = sem("y_turned")
        y_added = sem("y_added")
        NW = 8

        def schedule(eng, norm, prepare, start, states):
            for b in range(2):
                for n in sorted(norm):
                    norm[n](b, b)
                if b == 0:
                    for n in sorted(prepare):
                        prepare[n](0, 0)
            start()
            states(0, 0, True, True)
            with eng.Fori(0, (B - 4) // 2) as it:
                for par in range(2):
                    states(2 * it + 1 + par, 1 - par, True, True)
            states(B - 3, 1, True, True)
            states(B - 2, 0, True, False)
            states(B - 1, 1, False, False)

        def between(n, b, par, nxt, more, norm, prepare):
            if nxt and n in prepare:
                prepare[n](b + 1, 1 - par)
            if more and n in norm:
                norm[n](b + 2, par)

        block = ctx.enter_context(nc.Block())

        @block.sync
        def _(sp):
            by_half = "(c p) n -> p c n"
            sp.dma_start(convw[:, :, :], d["conv_w"].rearrange(by_half, p=P)).then_inc(w_in, 16)
            sp.dma_start(convb[:, :], d["conv_b"]).then_inc(w_in, 16)
            sp.dma_start(wdt[:, :, :], d["x_proj_dt_w"].rearrange(by_half, p=P)).then_inc(w_in, 16)
            sp.dma_start(wdt2[:, :], d["dt_proj_w"]).then_inc(w_in, 16)
            sp.dma_start(dtb[:, :], d["dt_proj_b"]).then_inc(w_in, 16)
            sp.dma_start(wbc[:, :, :], d["BC_proj_w"].rearrange(by_half, p=P)).then_inc(w_in, 16)
            sp.dma_start(A[:, :, :], d["A_log"].rearrange(by_half, p=P)).then_inc(w_in, 16)
            sp.dma_start(D[:, :], d["D_param"]).then_inc(w_in, 16)

        @block.gpsimd
        def _(pool):
            def soft(b, par):
                pool.wait_ge(log_z, b + 1)
                if not isinstance(b, int) or b >= 2:
                    pool.wait_ge(dA_ready, NS * (b - 1))
                    pool.wait_ge(dBx_ready, NS * (b - 1))
                nc.gpsimd.tensor_tensor(up[:, :, :], up[:, :, :], ones, ALU.subtract).then_inc(soft_step, 1)
                pool.wait_ge(soft_step, 3 * b + 1)
                nc.gpsimd.tensor_tensor(ez[:, :, :], ez[:, :, :], up[:, :, :], ALU.subtract).then_inc(soft_step, 1)
                pool.wait_ge(soft_step, 3 * b + 2)
                nc.gpsimd.tensor_tensor(mag[:, :, :], mag[:, :, :], ez[:, :, :], ALU.add).then_inc(soft_step, 1)
                pool.wait_ge(soft_step, 3 * b + 3)
                nc.gpsimd.tensor_tensor(dt[par][:, :, :], mag[:, :, :], pos[:, :, :], ALU.add).then_inc(dt_ready, 1)
                pool.wait_ge(dt_ready, b + 1)
                nc.gpsimd.tensor_tensor(dtx[par][:, :, :], dt[par][:, :, :], xc[par][:, :, :], ALU.mult).then_inc(dtx_ready, 1)

            def split(b, par):
                pool.wait_ge(bc_copied, b + 1)
                nc.gpsimd.tensor_tensor(bc32[:, :], bc32[:, :], bcs[par][:, :], ALU.subtract).then_inc(bc_rest1, 1)
                pool.wait_ge(bc_part2, b + 1)
                r = slice(2 * BCR, 3 * BCR)
                nc.gpsimd.tensor_tensor(bcs[par][r], bc32[r], bcs[par][r], ALU.subtract).then_inc(bc_ready, 1)
                pool.wait_ge(bc_ready, b + 1)

            prepare = {0: split, 1: soft}

            def states(b, par, nxt, more):
                for n in range(2):
                    between(n, b, par, nxt, more, {}, prepare)

            schedule(pool, {}, prepare, lambda: None, states)

        @block.scalar
        def _(act):
            nc.scalar.preload_act_table_set(LN_EXP)
            act.wait_ge(w_in, 16 * NW)
            nc.scalar.activation(A[:, :, :], A[:, :, :], ACT.Exp).then_inc(a_exp, 1)

            def inv_std(b, par):
                act.wait_ge(var_ready, b + 1)
                nc.scalar.activation(lnvar[:, :], mv[:, :, 1], ACT.Ln, bias=eps[:, 0:1]).then_inc(ln_done, 1)
                act.wait_ge(ln_done, b + 1)
                nc.scalar.activation(rstd[:, :], lnvar[:, :], ACT.Exp, scale=-0.5).then_inc(rstd_ready, 1)

            def turn(b, par):
                for c in range(HC):
                    act.wait_ge(turned, HC * b + c + 1)
                    nc.scalar.copy(xp[:, c, TAPS - 1:], pp[c][:, :]).then_inc(xp_ready, 1)

            def conv(b, par):
                if not isinstance(b, int) or b >= 2:
                    act.wait_ge(y_ready, b - 1)
                    act.wait_ge(dtx_ready, b - 1)
                for c in range(HC):
                    act.wait_ge(conv_done, HC * b + c + 1)
                    nc.scalar.activation(xc[par][:, c, :], pp[c][:, :], ACT.Silu, bias=convb[:, c:c + 1]).then_inc(xc_ready, 1)
                nc.scalar.preload_act_table_set(LN_EXP)

            def low_rank(b, par):
                act.wait_ge(low_done, b + 1)
                nc.scalar.copy(low[:, :], pp[0][0:RANK, :]).then_inc(low_ready, 1)
                act.wait_ge(bc_done, b + 1)
                if not isinstance(b, int) or b >= 2:
                    act.wait_ge(spread_C, NS * (b - 1))
                if not isinstance(b, int) or b >= 1:
                    act.wait_ge(bc_ready, b)
                nc.scalar.copy(bcs[par][:, :], pp[1][0:SPLITS * BCR, :])
                nc.scalar.copy(bc32[:, :], pp[1][0:SPLITS * BCR, :]).then_inc(bc_copied, 1)

            def second_part(b, par):
                act.wait_ge(bc_rest1, b + 1)
                nc.scalar.copy(bcs[par][BCR:2 * BCR], bc32[BCR:2 * BCR])
                nc.scalar.copy(bcs[par][2 * BCR:3 * BCR], bc32[2 * BCR:3 * BCR]).then_inc(bc_part2, 1)

            def softplus(b, par):
                if not isinstance(b, int) or b >= 1:
                    act.wait_ge(dt_ready, b)
                for c in range(HC):
                    act.wait_ge(z_done, HC * b + c + 1)
                    nc.scalar.activation(mag[:, c, :], pp[c][:, :], ACT.Abs, bias=dtb[:, c:c + 1])
                    nc.scalar.activation(pos[:, c, :], pp[c][:, :], ACT.Relu, bias=dtb[:, c:c + 1]).then_inc(z_read, 1)
                act.wait_ge(z_read, HC * (b + 1))
                nc.scalar.activation(ez[:, :, :], mag[:, :, :], ACT.Exp, scale=-1.0).then_inc(exp_z, 1)
                act.wait_ge(exp_z, b + 1)
                nc.scalar.activation(up[:, :, :], ez[:, :, :], ACT.Identity, bias=1.0).then_inc(one_z, 1)
                act.wait_ge(one_z, b + 1)
                nc.scalar.activation(mag[:, :, :], up[:, :, :], ACT.Ln).then_inc(log_z, 1)

            norm = {14: inv_std}
            prepare = {4: turn, 7: conv, 9: low_rank, 10: second_part, 11: softplus}

            def states(b, par, nxt, more):
                act.wait_ge(dt_ready, b + 1)
                for n in range(NS):
                    g = NS * b + n
                    if n >= 2 or not isinstance(b, int) or b >= 1:
                        act.wait_ge(scanned, g - 1)
                    for c in range(HC):
                        last = nc.scalar.activation(dA[n % 2][:, c, 1:], dt[par][:, c, 1:], ACT.Exp, scale=A[:, c, n:n + 1])
                    last.then_inc(dA_ready, 1)
                    between(n, b, par, nxt, more, norm, prepare)

            act.wait_ge(setup, 1)
            schedule(act, norm, prepare, lambda: None, states)

        @block.vector
        def _(dve):
            nc.vector.memset(xp[:, :, 0:TAPS - 1], 0.0)
            for i in range(2):
                nc.vector.memset(dA[i][:, :, 0:1], 0.0)
            dve.wait_ge(w_in, 16 * NW)
            for c in range(HC):
                for k in range(TAPS):
                    nc.vector.tensor_scalar(taps[:, c, k, :], ident, convw[:, c, k:k + 1], None, ALU.mult)
            dve.wait_ge(a_exp, 1)
            nc.vector.tensor_scalar(A[:, :, :], A[:, :, :], -1.0, None, ALU.mult).then_inc(setup, 1)

            def norm_stats(b, par):
                for i in range(QT):
                    last = nc.vector.bn_stats(stats[:, i, :], x[:, QT * b + i, :])
                last.then_inc(stat_done, 1)
                dve.wait_ge(stat_done, b + 1)
                nc.vector.memset(pause[:, :], 0.0)
                for i in range(QT):
                    last = nc.vector.bn_aggr(mv[:, i, :], stats[:, i, :])
                last.then_inc(var_ready, 1)

            def normalize(b, par):
                dve.wait_ge(rstd_ready, b + 1)
                if not isinstance(b, int) or b >= 1:
                    dve.wait_ge(turned, HC * b)
                for i in range(QT):
                    last = nc.vector.tensor_scalar(xh[:, i, :], x[:, QT * b + i, :], mv[:, i, 0:1], rstd[:, i:i + 1],
                                                   ALU.subtract, ALU.mult)
                last.then_inc(xh_ready, 1)

            norm = {11: norm_stats, 15: normalize}

            def both(bank):
                return bank[:, :].rearrange("p (a t) -> p a t", a=1).to_broadcast([P, HC, S])

            def drive(b, par, n):
                g = NS * b + n
                if n == 0:
                    dve.wait_ge(dtx_ready, b + 1)
                dve.wait_ge(spread_B, g + 1)
                nc.vector.tensor_tensor(dBx[n % 2][:, :, :], dtx[par][:, :, :], both(bB[n % 2]), ALU.mult).then_inc(dBx_ready, 1)

            def scan(b, par, n):
                g = NS * b + n
                dve.wait_ge(dBx_ready, g + 1)
                dve.wait_ge(dA_ready, g + 1)
                flat = "p c t -> p (c t)"
                nc.vector.tensor_tensor_scan(hs[n % 2][:, :, :].rearrange(flat), dA[n % 2][:, :, :].rearrange(flat),
                                             dBx[n % 2][:, :, :].rearrange(flat), 0.0, ALU.mult, ALU.add).then_inc(scanned, 1)

            def read(b, par, n):
                g = NS * b + n
                dve.wait_ge(scanned, g + 1)
                dve.wait_ge(spread_C, g + 1)
                if n >= 2 or not isinstance(b, int) or b >= 1:
                    dve.wait_ge(summed, g - 1)
                nc.vector.tensor_tensor(hC[n % 2][:, :, :], hs[n % 2][:, :, :], both(bC[n % 2]), ALU.mult).then_inc(hC_ready, 1)

            def start():
                drive(0, 0, 0)
                scan(0, 0, 0)

            def states(b, par, nxt, more):
                for n in range(NS):
                    if n:
                        drive(b, par, n)
                        scan(b, par, n)
                    read(b, par, n)
                    between(n, b, par, nxt, more, norm, {})
                if nxt:
                    drive(b + 1, 1 - par, 0)
                dve.wait_ge(summed, NS * (b + 1))
                if not isinstance(b, int) or b >= 1:
                    dve.wait_ge(y_turned, HC * b)
                for c in range(HC):
                    last = nc.vector.scalar_tensor_tensor(out=yT[:, c, :], in0=xc[par][:, c, :], scalar=D[:, c:c + 1],
                                                          in1=yp[:, c, :], op0=ALU.mult, op1=ALU.add)
                last.then_inc(y_ready, 1)
                if nxt:
                    scan(b + 1, 1 - par, 0)
                for c in range(HC):
                    dve.wait_ge(y_turned, HC * b + c + 1)
                    xb = x[:, bass.ds(QT * b, QT), c * P:(c + 1) * P]
                    nc.vector.tensor_tensor(xb, xb, pp[c][:, :].rearrange("p (i e) -> p i e", i=QT), ALU.add).then_inc(y_added, 1)

            schedule(dve, norm, {}, start, states)

        @block.tensor
        def _(pe):
            def turn(b, par):
                pe.wait_ge(xh_ready, b + 1)
                if not isinstance(b, int) or b >= 2:
                    pe.wait_ge(y_added, HC * (b - 1))
                elif b == 1:
                    pe.wait_ge(z_read, HC)
                for c in range(HC):
                    for i in range(QT):
                        last = nc.tensor.transpose(pp[c][:, i * P:(i + 1) * P], xh[:, i, c * P:(c + 1) * P], ident)
                    last.then_inc(turned, 1)

            def conv(c):
                def step(b, par):
                    pe.wait_ge(xp_ready, HC * (b + 1))
                    for k in range(TAPS):
                        last = nc.tensor.matmul(pp[c][:, :], taps[:, c, k, :], xp[:, c, k:k + S], start=k == 0, stop=k == TAPS - 1)
                    last.then_inc(conv_done, 1)
                return step

            def low_rank(b, par):
                pe.wait_ge(xc_ready, HC * (b + 1))
                for c in range(HC):
                    last = nc.tensor.matmul(pp[0][0:RANK, :], wdt[:, c, :], xc[par][:, c, :], start=c == 0, stop=c == HC - 1)
                last.then_inc(low_done, 1)
                for c in range(HC):
                    last = nc.tensor.matmul(pp[1][0:SPLITS * BCR, :], wbc[:, c, :], xc[par][:, c, :], start=c == 0, stop=c == HC - 1)
                last.then_inc(bc_done, 1)

            def zed(b, par):
                pe.wait_ge(low_ready, b + 1)
                pe.wait_ge(bc_copied, b + 1)
                for c in range(HC):
                    nc.tensor.matmul(pp[c][:, :], wdt2[:, c * P:(c + 1) * P], low[:, :], start=True, stop=True).then_inc(z_done, 1)

            prepare = {1: turn, 4: conv(0), 5: conv(1), 7: low_rank, 9: zed}

            def spread(b, par, n):
                g = NS * b + n
                if n == 0:
                    pe.wait_ge(bc_ready, b + 1)
                if n >= 2 or not isinstance(b, int) or b >= 1:
                    pe.wait_ge(dBx_ready, g - 1)
                sel = cb[0:SPLITS * BCR, CB_SEL + n * P:CB_SEL + (n + 1) * P]
                nc.tensor.matmul(bB[n % 2][:, :], sel, bcs[par][:, :], start=True, stop=True).then_inc(spread_B, 1)
                if n >= 2 or not isinstance(b, int) or b >= 1:
                    pe.wait_ge(hC_ready, g - 1)
                sel = cb[0:SPLITS * BCR, CB_SEL + (NS + n) * P:CB_SEL + (NS + n + 1) * P]
                nc.tensor.matmul(bC[n % 2][:, :], sel, bcs[par][:, :], start=True, stop=True).then_inc(spread_C, 1)

            def add_up(b, par, n):
                g = NS * b + n
                pe.wait_ge(hC_ready, g + 1)
                if n == 0 and (not isinstance(b, int) or b >= 1):
                    pe.wait_ge(y_ready, b)
                for c in range(HC):
                    last = nc.tensor.matmul(yp[:, c, :], ident, hC[n % 2][:, c, :], start=n == 0, stop=n == NS - 1)
                last.then_inc(summed, 1)

            def states(b, par, nxt, more):
                for n in range(NS):
                    if n < NS - 1:
                        spread(b, par, n + 1)
                    elif nxt:
                        spread(b + 1, 1 - par, 0)
                    add_up(b, par, n)
                    between(n, b, par, nxt, more, {}, prepare)
                pe.wait_ge(y_ready, b + 1)
                if nxt:
                    pe.wait_ge(z_read, HC * (b + 2))
                else:
                    pe.wait_ge(y_added, HC * b)
                for c in range(HC):
                    for i in range(QT):
                        last = nc.tensor.transpose(pp[c][:, i * P:(i + 1) * P], yT[:, c, i * P:(i + 1) * P], ident)
                    last.then_inc(y_turned, 1)

            pe.wait_ge(w_in, 16 * NW)
            pe.wait_ge(setup, 1)
            schedule(pe, {}, prepare, lambda: spread(0, 0, 0), states)


def build_ffn(nc, sems, tag, x, cf, eps, weights_in, xs, ys, zeros, pool_dmas, out=None):
    router_in, w1_in, w3_in, w2_in = weights_in
    scattered, stored, fetched = pool_dmas
    with ExitStack() as ctx:
        def sb(name, shape, dt=F32):
            return ctx.enter_context(nc.sbuf_tensor(f"{tag}_{name}", shape, dt))

        w1 = sb("w1", [P, E, HC, F])
        w3 = sb("w3", [P, E, HC, F])
        w2 = sb("w2", [P, E, FC, H])
        router = sb("router", [P, HC, E])
        slots = [sb(f"slots{c}", [P, NT], I32) for c in range(2)]
        weights = [sb(f"weights{c}", [P, NT]) for c in range(2)]
        tile_expert = sb("tile_expert", [P, MTILES], I32)
        w_in = sems.enter_context(nc.semaphore(f"{tag}_w_in"))
        r_in = sems.enter_context(nc.semaphore(f"{tag}_r_in"))
        with nc.Block() as block:
            @block.sync
            def _(sp):
                sp.dma_start(router[:, :, :], router_in.rearrange("(c p) e -> p c e", p=P)).then_inc(r_in, 16)
                for w, w_dram in ((w1, w1_in), (w3, w3_in), (w2, w2_in)):
                    for e in range(E):
                        sp.dma_start(w[:, e], w_dram[e].rearrange("(c p) f -> p c f", p=P)).then_inc(w_in, 16)
                sp.wait_ge(r_in, 16)
                if zeros is not None:
                    sp.wait_ge(*zeros)
        with ExitStack() as inner:
            xh = inner.enter_context(nc.sbuf_tensor(f"{tag}_xh", [P, NT, H], F32))
            build_route(nc, sems, tag, x, xh, cf, eps, router, xs, slots, weights, tile_expert, scattered)
        build_experts(nc, sems, tag, cf, w1, w3, w2, [(w_in, 16 * 3 * E)], xs, ys, tile_expert, stored)
        build_combine(nc, sems, tag, x, ys, slots, weights, fetched, out)


def build_layers(nc, hidden, cf_in, cb_in, attention_in, mamba_in, ffn_in, out):
    token_major = "(t p) h -> p t h"
    x_in = hidden.rearrange("b s h -> (b s) h").rearrange(token_major, p=P)
    x_out = out.rearrange("b s h -> (b s) h").rearrange(token_major, p=P)
    xs = nc.dram_tensor("expert_rows_in", [MTILES * P, H], F32).ap()
    ys = nc.dram_tensor("expert_rows_out", [MTILES * P, H], F32).ap()
    ZT = 8
    with ExitStack() as sems, ExitStack() as ctx:
        x = ctx.enter_context(nc.sbuf_tensor("x", [P, NT, H], F32))
        cf = ctx.enter_context(nc.sbuf_tensor("cf", [P, CF_N], F32))
        cb = ctx.enter_context(nc.sbuf_tensor("cb", [P, CB_N], BF16))
        eps = ctx.enter_context(nc.sbuf_tensor("eps", [P, 1], F32))
        zero = ctx.enter_context(nc.sbuf_tensor("zero", [P, 1, H], F32))
        x_loaded = sems.enter_context(nc.semaphore("x_loaded"))
        zeroed = sems.enter_context(nc.semaphore("zeroed"))
        cleared = sems.enter_context(nc.semaphore("cleared"))
        pool_dmas = [(sems.enter_context(nc.semaphore(f"scattered_{tag}")),
                      [sems.enter_context(nc.semaphore(f"stored_{tag}_{i}")) for i in range(LB)],
                      [sems.enter_context(nc.semaphore(f"fetched_{tag}_{i}")) for i in range(RB)]) for tag in ("f1", "f2")]
        with nc.Block() as block:
            @block.sync
            def _(sp):
                sp.dma_start(x[:, :, :], x_in).then_inc(x_loaded, 16)
                sp.dma_start(cf[:, :], cf_in).then_inc(x_loaded, 16)
                sp.dma_start(cb[:, :], cb_in).then_inc(x_loaded, 16)
                sp.wait_ge(zeroed, 1)
                for t in range(0, MTILES, ZT):
                    sp.dma_start(xs[t * P:(t + ZT) * P].rearrange(token_major, p=P),
                                 zero[:, :, :].to_broadcast([P, ZT, H])).then_inc(cleared, 16)
                sp.wait_ge(x_loaded, 48)

            @block.vector
            def _(dve):
                nc.vector.memset(eps[:, :], EPS)
                nc.vector.memset(zero[:, :, :], 0.0).then_inc(zeroed, 1)
        with ExitStack() as attention_sems:
            used = build_attention(nc, attention_sems, x, cf, cb, attention_in, eps)
            with nc.Block() as block:
                @block.gpsimd
                def _(pool):
                    for s in used:
                        pool.sem_clear(s)
        build_ffn(nc, sems, "f1", x, cf, eps, ffn_in, xs, ys, (cleared, 16 * MTILES // ZT), pool_dmas[0])
        build_mamba(nc, sems, x, cf, cb, mamba_in, eps)
        build_ffn(nc, sems, "f2", x, cf, eps, ffn_in, xs, ys, None, pool_dmas[1], x_out)


def _tables(np, bf16):
    i = np.arange(P)
    cf = np.zeros((P, CF_N), np.float32)
    cf[:, CF_ID:CF_ID + P] = np.eye(P)
    cf[:, CF_TRI:CF_TRI + P] = i[:, None] < i[None, :]
    cf[:, CF_ONE:CF_ONE + P] = 1
    cf[:, CF_IOTA:CF_IOTA + NT * E] = np.tile(np.arange(E) - E, NT)
    cf[:, CF_SCAN:CF_SCAN + NT * E] = np.tile(np.arange(NT) > 0, E)
    cf[:, CF_TB:CF_TB + MTILES * E] = np.repeat(np.arange(MTILES) * P, E)
    cb = np.zeros((P, CB_N), bf16)
    cb[:, CB_ID:CB_ID + P] = np.eye(P)
    cb[:, CB_MT:CB_MT + P] = np.where(i[:, None] > i[None, :], MASKED, 0)
    cb[:, CB_MR:CB_MR + P] = np.where(i[None, :] > i[:, None], MASKED, 0)
    for r in range(BCR):
        for s in range(SPLITS):
            cb[s * BCR + r, CB_SEL + r * P:CB_SEL + (r + 1) * P] = 1
    return cf, cb


def kernel(**inputs):
    import ml_dtypes as _ml
    import numpy as _np
    import concourse.bacc as _bacc
    from concourse import mybir as _mybir
    from concourse.bass_utils import run_bass_kernel_spmd as _run

    a = {k: _np.asarray(v) for k, v in inputs.items()}

    def by_half(v):
        return v.reshape(HC, P).T

    at = {k: a["L0_attn_a_" + k] for k in ("Wq", "bq", "Wk", "bk", "Wv", "bv", "Wo", "bo")}
    ma = {k: a["L0_attn_b_" + k] for k in ("conv_w", "conv_b", "x_proj_dt_w", "dt_proj_w", "dt_proj_b",
                                           "B_proj_w", "C_proj_w", "A_log", "D_param")}
    cf, cb = _tables(_np, _ml.bfloat16)
    attention = {k: at[k].T for k in ("Wq", "Wk", "Wv", "Wo")}
    attention.update(bqk=_np.concatenate([at["bq"], at["bk"]]).reshape(2 * HC, P).T, bv=at["bv"], bo=at["bo"])
    mamba = {
        "conv_w": ma["conv_w"][:, 0], "conv_b": by_half(ma["conv_b"]), "x_proj_dt_w": ma["x_proj_dt_w"].T,
        "dt_proj_w": ma["dt_proj_w"].T, "dt_proj_b": by_half(ma["dt_proj_b"]),
        "BC_proj_w": _np.concatenate([ma["B_proj_w"], ma["C_proj_w"]] * SPLITS, 0).T,
        "A_log": ma["A_log"], "D_param": by_half(ma["D_param"]),
    }
    ffn = {k: a["L0_ffn_" + k] for k in ("router_w", "w1", "w3", "w2")}

    nc = _bacc.Bacc("TRN2", target_bir_lowering=False, num_devices=1)
    arrays = {}

    def dram(name, v):
        v = _np.ascontiguousarray(v)
        arrays[f"in_{name}_dram"] = v
        return nc.dram_tensor(f"in_{name}_dram", v.shape, _mybir.dt.from_np(v.dtype), kind="ExternalInput").ap()

    hidden_in = dram("hidden", a["L0_attn_a_hidden_states"])
    cf_in, cb_in = dram("cf", cf), dram("cb", cb)
    attention_in = {k: dram(k, v) for k, v in attention.items()}
    mamba_in = {k: dram(k, v) for k, v in mamba.items()}
    ffn_in = [dram(k, v) for k, v in ffn.items()]
    out = nc.dram_tensor("out_0_dram", (B, S, H), _mybir.dt.from_np(_np.dtype("float32")), kind="ExternalOutput").ap()
    build_layers(nc, hidden_in, cf_in, cb_in, attention_in, mamba_in, ffn_in, out)
    r = _run(nc, [arrays], core_ids=[0])
    return r.results[0]["out_0_dram"]
```

```python
from contextlib import ExitStack

import concourse.bass as bass
from concourse import mybir

F32 = mybir.dt.float32
BF16 = mybir.dt.bfloat16
I32 = mybir.dt.int32
ALU = mybir.AluOpType
ACT = mybir.ActivationFunctionType
AX = mybir.AxisListType

P = 128
B, S, H = 8, 512, 256
NH, HD = 16, 16
T = B * S
NT = T // P
QT = S // P
HC = H // P
E, F = 8, 512
FC = F // P
EPS = 1e-5
SPLITS = 3
PAIRS = ((0, 0), (0, 1), (1, 0), (1, 1), (0, 2), (2, 0))
KROWS = len(PAIRS) * HD
MROWS = KROWS + SPLITS
ROUTED = 2 * T
CAP = T + P
MTILES = ROUTED // P + E - 1
MTILES += MTILES % 2
SPARE = MTILES - ROUTED // P
ROWS = E * CAP + SPARE * P
LB = 4
RB = 8
NS, RANK, TAPS = 16, 64, 4
BCR = 2 * NS
MASKED = -1e30
BIG = 3.0e38
LN_EXP = 'natural_log_exp_and_others'
MAGIC = 12582912.0

CF_ID, CF_TRI, CF_ONE = 0, P, 2 * P
CF_IOTA = 3 * P
CF_FRESH = CF_IOTA + QT * E
CF_REGION = CF_FRESH + QT * E
CF_PART = CF_REGION + E
CF_TB = CF_PART + 1
CF_N = CF_TB + MTILES * E
CB_ID, CB_MT, CB_MR, CB_SEL = 0, 128, 256, 384
CB_N = CB_SEL + BCR * P


def rows(v, n):
    return v.rearrange("(a n) -> a n", a=1).to_broadcast([P, n])


def build_attention(nc, sems, x, cf, cb, d, eps, way, rest, x_rest):
    ident = cf[:, CF_ID:CF_ID + P]
    ident_b = cb[:, CB_ID:CB_ID + P]
    mask_t = cb[:, CB_MT:CB_MT + P]
    mask_r = cb[:, CB_MR:CB_MR + P]
    KOFF = [0, 512, 896, 1152]
    PTW = 1280
    HG = 32
    with ExitStack() as ctx:
        def sb(name, shape, dt=F32):
            return ctx.enter_context(nc.sbuf_tensor(name, shape, dt))

        def ps(name, shape):
            return ctx.enter_context(nc.psum_tensor(name, shape, F32))

        used = []

        def sem(name):
            used.append(sems.enter_context(nc.semaphore(name)))
            return used[-1]

        wqkvo = sb("wqkvo", [P, 4, HC, H])
        qkbias = sb("qkbias", [P, 4])
        vbias = sb("vbias", [P, H])
        obias = sb("obias", [P, H])
        stats = sb("at_stats", [P, QT, 6])
        mv = sb("at_mv", [P, QT, 2])
        lnvar = sb("at_lnvar", [P, QT])
        rstd = sb("at_rstd", [P, QT])
        pause = sb("at_pause", [P, 1])
        xh = sb("at_xh", [P, QT, H])
        xT = sb("at_xT", [P, HC, S])
        qk32 = sb("qk32", [P, 4, S])
        parts = sb("parts", [P, SPLITS, 4, S], BF16)
        KS = [sb(f"KS{i}", [MROWS, NH, S], BF16) for i in range(2)]
        QS = [sb(f"QS{i}", [MROWS, NH, S], BF16) for i in range(2)]
        V = [sb(f"V{i}", [P, QT, NH, HG]) for i in range(2)]
        rowmax = sb("rowmax", [P, QT, NH])
        m32 = sb("m32", [NH, S])
        mparts = sb("mparts", [NH, SPLITS, S], BF16)
        probs = [sb(f"probs{i}", [P, PTW]) for i in range(2)]
        recip = sb("recip", [P, 2, QT, 4])
        oT = sb("oT", [P, S])
        attn = sb("attn", [P, QT, H])
        attnT = sb("attnT", [P, HC, S])
        scr = nc.dram_tensor("qk_parts", [2, SPLITS, 4, P, S], BF16).ap()

        sc = [ps(f"sc{i}", [P, 512]) for i in range(3)]
        mx = [ps(f"mx{i}", [P, 512]) for i in range(2)]
        O = ps("O", [P, 512])
        misc = [ps(f"misc{i}", [P, 512]) for i in range(2)]

        w_in = sem("w_in")
        ones_set = sem("ones_set")
        stat_done = sem("stat_done")
        var_ready = sem("var_ready")
        ln_done = sem("ln_done")
        rstd_ready = sem("rstd_ready")
        xh_ready = sem("xh_ready")
        xT_psum = sem("xT_psum")
        xT_ready = sem("xT_ready")
        qk_psum = sem("qk_psum")
        qk_evac = sem("qk_evac")
        qk_rest1 = sem("qk_rest1")
        qk_part2 = sem("qk_part2")
        qk_part3 = sem("qk_part3")
        parts_out = sem("parts_out")
        stacked = sem("stacked")
        v_psum = sem("v_psum")
        v_evac = sem("v_evac")
        mx_psum = sem("mx_psum")
        mx_read = sem("mx_read")
        mT_psum = sem("mT_psum")
        mT_evac = sem("mT_evac")
        m_rest1 = sem("m_rest1")
        m_part2 = sem("m_part2")
        m_part3 = sem("m_part3")
        m_stacked = sem("m_stacked")
        sc_psum = sem("sc_psum")
        exp_done = sem("exp_done")
        pv_done = sem("pv_done")
        oT_evac = sem("oT_evac")
        o_turned = sem("o_turned")
        recip_done = sem("recip_done")
        o_read = sem("o_read")
        aT_psum = sem("aT_psum")
        aT_evac = sem("aT_evac")
        wo_psum = sem("wo_psum")
        wo_sum = sem("wo_sum")
        wo_evac = sem("wo_evac")
        NW = 7

        way.begin(sems, ctx, [misc[1], misc[0]], misc[0], attnT)

        def schedule(eng, norm, project, values, maxima, attend):
            for b in range(2):
                norm(b)
                project(b, b)
                values(b, b)
            maxima(0, 0)
            attend(0, 0, True, True)
            with eng.Fori(0, (B - 4) // 2) as it:
                for par in range(2):
                    attend(2 * it + 1 + par, 1 - par, True, True)
            attend(B - 3, 1, True, True)
            attend(B - 2, 0, True, False)
            attend(B - 1, 1, False, False)

        SPLIT_SLOTS = (13, 14, 15)
        NORM_SLOT, XT_SLOT, Q_SLOT, K_SLOT = 5, 10, 11, 12
        units = [(h + j, n, i) for h in range(0, NH, 4) for i, n in enumerate((4, 2, 1, 1)) for j in range(0, 4, n)]
        FIRST_SLOT, PER_SLOT = 5, 5
        MAXIMA_SLOT = 14

        def unit_range(slot):
            if slot < FIRST_SLOT:
                return range(0)
            a = (slot - FIRST_SLOT) * PER_SLOT
            return range(a, min(a + PER_SLOT, len(units)))

        block = ctx.enter_context(nc.Block())

        @block.sync
        def _(sp):
            for i, w in enumerate(("Wq", "Wk", "Wv", "Wo")):
                sp.dma_start(wqkvo[:, i], d[w].rearrange("(c p) n -> p c n", p=P)).then_inc(w_in, 16)
            sp.dma_start(qkbias[:, :], d["bqk"]).then_inc(w_in, 16)
            sp.dma_start(vbias[:, :], rows(d["bv"], H)).then_inc(w_in, 16)
            sp.dma_start(obias[:, :], rows(d["bo"], H)).then_inc(w_in, 16)
            for to, source in rest:
                sp.dma_start(to, source).then_inc(x_rest, 16)

            def store_parts(b, par):
                split, read = b + 1, 16 * 12 * (b - 1)
                sp.compute_val(read)
                sp.wait_ge(qk_part3, split)
                if not isinstance(b, int) or b >= 2:
                    sp.wait_ge(stacked, read)
                sp.dma_start(scr[par].rearrange("s j p t -> p s j t"), parts[:, :, :, :]).then_inc(parts_out, 16)

            def stack(b, par):
                written, used = 16 * (b + 1), NH * (b - 1)
                sp.compute_val(used)
                sp.wait_ge(parts_out, written)
                if not isinstance(b, int) or b >= 2:
                    sp.wait_ge(pv_done, used)
                for n, (kp, qp) in enumerate(PAIRS):
                    r = slice(HD * n, HD * n + HD)
                    sp.dma_start(QS[par][r], scr[par, qp, 0:2].rearrange("m (g e) t -> e (m g) t", e=HD)).then_inc(stacked, 16)
                    sp.dma_start(KS[par][r], scr[par, kp, 2:4].rearrange("m (g e) t -> e (m g) t", e=HD)).then_inc(stacked, 16)

            def maxima(b, par):
                sp.wait_ge(m_part3, b + 1)
                for s in range(SPLITS):
                    sp.dma_start(QS[par][KROWS + s:KROWS + s + 1], mparts[:, s, :]).then_inc(m_stacked, 16)

            def norm(b):
                pass

            def project(b, par):
                store_parts(b, par)
                stack(b, par)

            def values(b, par):
                pass

            def attend(b, par, nxt, more):
                if nxt:
                    maxima(b + 1, 1 - par)
                if more:
                    store_parts(b + 2, par)
                    stack(b + 2, par)

            schedule(sp, norm, project, values, maxima, attend)

        @block.gpsimd
        def _(pool):
            def norm(b):
                pass

            def project(b, par):
                pass

            def values(b, par):
                pass

            def maxima(b, par):
                pool.wait_ge(mT_evac, b + 1)
                nc.gpsimd.tensor_tensor(m32[:, :], m32[:, :], mparts[:, 0, :], ALU.subtract).then_inc(m_rest1, 1)
                pool.wait_ge(m_part2, b + 1)
                nc.gpsimd.tensor_tensor(mparts[:, 2, :], m32[:, :], mparts[:, 1, :], ALU.subtract).then_inc(m_part3, 1)

            def attend(b, par, nxt, more):
                if not isinstance(b, int) or b >= 1:
                    way.scatter(pool, b - 1, 1 - par)
                if nxt:
                    maxima(b + 1, 1 - par)

            way.start_pool(pool)
            schedule(pool, norm, project, values, maxima, attend)
            way.scatter(pool, B - 1, (B - 1) % 2)

        @block.scalar
        def _(act):
            def norm(b):
                act.wait_ge(var_ready, b + 1)
                nc.scalar.activation(lnvar[:, :], mv[:, :, 1], ACT.Ln, bias=eps[:, 0:1]).then_inc(ln_done, 1)
                act.wait_ge(ln_done, b + 1)
                nc.scalar.activation(rstd[:, :], lnvar[:, :], ACT.Exp, scale=-0.5).then_inc(rstd_ready, 1)

            def turned(b):
                for c in range(HC):
                    act.wait_ge(xT_psum, HC * b + c + 1)
                    nc.scalar.copy(xT[:, c, :], misc[1 - c][:, :]).then_inc(xT_ready, 1)

            def queries_keys(b, js):
                if not isinstance(b, int) or b >= 1:
                    act.wait_ge(qk_part3, b)
                    act.wait_ge(parts_out, 16 * b)
                for j in js:
                    act.wait_ge(qk_psum, 4 * b + j + 1)
                    nc.scalar.activation(parts[:, 0, j, :], misc[1 - j % 2][:, :], ACT.Identity, bias=qkbias[:, j:j + 1])
                    nc.scalar.activation(qk32[:, j, :], misc[1 - j % 2][:, :], ACT.Identity, bias=qkbias[:, j:j + 1]).then_inc(qk_evac, 1)

            def project(b, par):
                turned(b)
                queries_keys(b, range(4))

            def values(b, par):
                pass

            def first_part(b):
                act.wait_ge(mT_psum, b + 1)
                if not isinstance(b, int) or b >= 1:
                    act.wait_ge(m_stacked, 16 * SPLITS * b)
                nc.scalar.mul(mparts[:, 0, :], misc[0][0:NH, :], -1.0)
                nc.scalar.mul(m32[:, :], misc[0][0:NH, :], -1.0).then_inc(mT_evac, 1)

            def second_part(b):
                act.wait_ge(m_rest1, b + 1)
                nc.scalar.copy(mparts[:, 1, :], m32[:, :]).then_inc(m_part2, 1)

            def maxima(b, par):
                first_part(b)
                second_part(b)

            def group_out(b, g):
                act.wait_ge(pv_done, NH * b + 4 * g + 4)
                if g or not isinstance(b, int) or b >= 1:
                    act.wait_ge(o_turned, NH // 4 * b + g)
                nc.scalar.copy(oT[:, :], O[:, :]).then_inc(oT_evac, 1)

            def attend(b, par, nxt, more):
                for h in range(NH):
                    if h >= 2:
                        act.wait_ge(pv_done, NH * b + h - 1)
                    elif not isinstance(b, int) or b >= 1:
                        act.wait_ge(pv_done, NH * b + h - 1)
                    for n, (c0, c1) in enumerate(((0, 512), (512, 896), (896, 1280))):
                        act.wait_ge(sc_psum, 3 * (NH * b + h) + n + 1)
                        nc.scalar.activation(probs[h % 2][:, c0:c1], sc[n][:, 0:c1 - c0], ACT.Exp,
                                             scale=HD ** -0.5).then_inc(exp_done, 1)
                    if h % 4 == 0 and h:
                        group_out(b, h // 4 - 1)
                    if more and h == NORM_SLOT:
                        norm(b + 2)
                    if more and h == XT_SLOT:
                        turned(b + 2)
                    if more and h == Q_SLOT:
                        queries_keys(b + 2, range(2))
                    if more and h == K_SLOT:
                        queries_keys(b + 2, range(2, 4))
                    if not isinstance(b, int) or b >= 1:
                        if h == 0:
                            way.inv_std(act, b - 1)
                        if h == 2:
                            way.turned_out(act, b - 1)
                    if nxt and h == MAXIMA_SLOT:
                        first_part(b + 1)
                    if nxt and h == MAXIMA_SLOT + 1:
                        second_part(b + 1)
                group_out(b, NH // 4 - 1)
                for c in range(HC):
                    act.wait_ge(aT_psum, HC * b + c + 1)
                    nc.scalar.copy(attnT[:, c, :], misc[1 - c][:, :]).then_inc(aT_evac, 1)

            nc.scalar.preload_act_table_set(LN_EXP)
            act.wait_ge(w_in, 16 * NW)
            schedule(act, norm, project, values, maxima, attend)
            way.inv_std(act, B - 1)
            way.turned_out(act, B - 1)

        @block.vector
        def _(dve):
            def norm_stats(b):
                if isinstance(b, int) and b == 1:
                    dve.wait_ge(x_rest, 16 * len(rest))
                for i in range(QT):
                    last = nc.vector.bn_stats(stats[:, i, :], x[:, QT * b + i, :])
                last.then_inc(stat_done, 1)
                dve.wait_ge(stat_done, b + 1)
                nc.vector.memset(pause[:, :], 0.0)
                for i in range(QT):
                    last = nc.vector.bn_aggr(mv[:, i, :], stats[:, i, :])
                last.then_inc(var_ready, 1)

            def normalize(b):
                dve.wait_ge(rstd_ready, b + 1)
                if not isinstance(b, int) or b >= 1:
                    dve.wait_ge(xT_psum, HC * b)
                for i in range(QT):
                    last = nc.vector.tensor_scalar(xh[:, i, :], x[:, QT * b + i, :], mv[:, i, 0:1], rstd[:, i:i + 1],
                                                   ALU.subtract, ALU.mult)
                last.then_inc(xh_ready, 1)

            def values(b, par):
                if not isinstance(b, int) or b >= 2:
                    dve.wait_ge(pv_done, NH * (b - 1))
                for n in range(2):
                    dve.wait_ge(v_psum, 2 * b + n + 1)
                    nc.vector.tensor_tensor(
                        V[par][:, 2 * n:2 * n + 2, :, 0:HD],
                        misc[1 - n][:, :].rearrange("p (i h e) -> p i h e", i=2, h=NH),
                        vbias[:, :].rearrange("p (a h e) -> p a h e", a=1, h=NH).to_broadcast([P, 2, NH, HD]),
                        ALU.add).then_inc(v_evac, 1)

            def unit(b, u):
                h, n, i = units[u]
                dve.wait_ge(mx_psum, len(units) * b + u + 1)
                nc.vector.tensor_reduce(rowmax[:, i, h:h + n], mx[u % 2][:, 0:n * (i + 1) * P].rearrange("p (h k) -> p h k", h=n),
                                        AX.X, ALU.max).then_inc(mx_read, 1)

            def split(b, step):
                if step == 0:
                    dve.wait_ge(qk_evac, 4 * (b + 1))
                    nc.vector.tensor_tensor(qk32[:, :, :], qk32[:, :, :], parts[:, 0, :, :], ALU.subtract).then_inc(qk_rest1, 1)
                elif step == 1:
                    dve.wait_ge(qk_rest1, b + 1)
                    nc.vector.tensor_copy(parts[:, 1, :, :], qk32[:, :, :]).then_inc(qk_part2, 1)
                else:
                    dve.wait_ge(qk_part2, b + 1)
                    nc.vector.tensor_tensor(parts[:, 2, :, :], qk32[:, :, :], parts[:, 1, :, :], ALU.subtract).then_inc(qk_part3, 1)

            def norm(b):
                norm_stats(b)
                normalize(b)

            def project(b, par):
                for step in range(3):
                    split(b, step)

            def maxima(b, par):
                for u in range(len(units)):
                    unit(b, u)

            def group(b, g):
                o = misc[g % 2][:, :].rearrange("p (i h e) -> p i h e", i=QT, h=4)
                dve.wait_ge(o_turned, NH // 4 * b + g + 1)
                if g == 0 and (not isinstance(b, int) or b >= 1):
                    dve.wait_ge(aT_psum, HC * b)
                nc.vector.reciprocal(recip[:, g % 2], o[:, :, :, HD]).then_inc(recip_done, 1)
                dve.wait_ge(recip_done, NH // 4 * b + g + 1)
                a = attn[:, :, 64 * g:64 * g + 64].rearrange("p i (h e) -> p i h e", h=4)
                nc.vector.tensor_tensor(a, o[:, :, :, 0:HD],
                                        recip[:, g % 2].rearrange("p i (h a) -> p i h a", a=1).to_broadcast([P, QT, 4, HD]),
                                        ALU.mult).then_inc(o_read, 1)

            def attend(b, par, nxt, more):
                for h in range(NH):
                    if nxt:
                        for u in unit_range(h):
                            unit(b + 1, u)
                    if h % 4 == 1 and h > 1:
                        group(b, h // 4 - 1)
                    if more and h == NORM_SLOT:
                        norm(b + 2)
                    if more and h in SPLIT_SLOTS:
                        split(b + 2, SPLIT_SLOTS.index(h))
                    if not isinstance(b, int) or b >= 1:
                        if h == 0:
                            dve.wait_ge(wo_sum, 2 * b)
                            nc.vector.memset(pause[:, :], 0.0)
                            way.stats(dve, b - 1)
                        if h == 1:
                            way.normalize(dve, b - 1, 1 - par)
                        if h == 3:
                            way.choose(dve, b - 1)
                        if h == 4:
                            way.place(dve, b - 1, 1 - par)
                group(b, NH // 4 - 1)
                for n in range(2):
                    dve.wait_ge(wo_psum, 2 * b + n + 1)
                    xb = x[:, bass.ds(QT * b + 2 * n, 2), :]
                    pair = misc[1 - n][:, :].rearrange("p (i e) -> p i e", i=2)
                    nc.vector.tensor_tensor(xb, xb, pair, ALU.add).then_inc(wo_evac, 1)
                    dve.wait_ge(wo_evac, 2 * b + n + 1)
                    nc.vector.tensor_tensor(
                        xb, xb, obias[:, :].rearrange("p (a e) -> p a e", a=1).to_broadcast([P, 2, H]),
                        ALU.add).then_inc(wo_sum, 1)
                if more:
                    values(b + 2, par)

            for i in range(2):
                nc.vector.memset(KS[i][KROWS:MROWS], 1.0).then_inc(ones_set, 1)
                nc.vector.memset(V[i][:, :, :, HD:HG], 0.0).then_inc(ones_set, 1)
                dve.wait_ge(ones_set, 3 * i + 2)
                nc.vector.memset(V[i][:, :, :, HD:HD + 1], 1.0).then_inc(ones_set, 1)
            dve.wait_ge(w_in, 16 * NW)
            way.start_dve(dve)
            schedule(dve, norm, project, values, maxima, attend)
            dve.wait_ge(wo_sum, 2 * B)
            way.stats(dve, B - 1)
            way.normalize(dve, B - 1, (B - 1) % 2)
            way.choose(dve, B - 1)
            way.place(dve, B - 1, (B - 1) % 2)

        @block.tensor
        def _(pe):
            def turn_tokens(b):
                pe.wait_ge(xh_ready, b + 1)
                if isinstance(b, int) and b < 2:
                    if b:
                        pe.wait_ge(v_evac, 2 * b)
                else:
                    pe.wait_ge(o_read, NH // 4 * (b - 2) + 2)
                for c in range(HC):
                    for i in range(QT):
                        last = nc.tensor.transpose(misc[1 - c][:, i * P:(i + 1) * P], xh[:, i, c * P:(c + 1) * P], ident)
                    last.then_inc(xT_psum, 1)

            def queries_keys(b, js):
                for j in js:
                    if j < 2:
                        pe.wait_ge(xT_ready, HC * b + 2)
                    else:
                        pe.wait_ge(qk_evac, 4 * b + j - 1)
                    for c in range(HC):
                        last = nc.tensor.matmul(misc[1 - j % 2][:, :], wqkvo[:, j // 2, c, (j % 2) * P:(j % 2 + 1) * P],
                                                xT[:, c, :], start=c == 0, stop=c == HC - 1)
                    last.then_inc(qk_psum, 1)

            def norm(b):
                pass

            def project(b, par):
                turn_tokens(b)
                queries_keys(b, range(4))

            def values(b, par):
                for n in range(2):
                    if isinstance(b, int) and b < 2:
                        pe.wait_ge(qk_evac, 4 * b + n + 3)
                    else:
                        pe.wait_ge(wo_evac, 2 * (b - 2) + n + 1)
                    for i in range(2):
                        for c in range(HC):
                            t = 2 * n + i
                            last = nc.tensor.matmul(misc[1 - n][:, i * H:(i + 1) * H], xT[:, c, t * P:(t + 1) * P],
                                                    wqkvo[:, 2, c, :], start=c == 0, stop=c == HC - 1)
                    last.then_inc(v_psum, 1)

            def unit(b, par, u):
                h0, n, i = units[u]
                if u >= 2 or not isinstance(b, int) or b >= 1:
                    pe.wait_ge(mx_read, len(units) * b + u - 1)
                w = (i + 1) * P
                for j in range(n):
                    nc.tensor.matmul(mx[u % 2][:, j * w:(j + 1) * w], QS[par][0:KROWS, h0 + j, i * P:w], KS[par][0:KROWS, h0 + j, 0:w],
                                     start=True, stop=False)
                    last = nc.tensor.matmul(mx[u % 2][:, j * w + i * P:(j + 1) * w], ident_b, mask_r, start=False, stop=True)
                last.then_inc(mx_psum, 1)

            def turn_maxima(b):
                pe.wait_ge(mx_read, len(units) * (b + 1))
                if isinstance(b, int) and b == 0:
                    pe.wait_ge(v_evac, 4)
                else:
                    pe.wait_ge(o_read, NH // 4 * b - 1)
                for i in range(QT):
                    last = nc.tensor.transpose(misc[0][0:NH, i * P:(i + 1) * P], rowmax[:, i, :], ident)
                last.then_inc(mT_psum, 1)

            def maxima(b, par):
                pe.wait_ge(stacked, 16 * 12 * (b + 1))
                for u in range(len(units)):
                    unit(b, par, u)
                turn_maxima(b)

            def scores(b, par, h, ahead):
                for n, kts in enumerate(((0,), (1,), (2, 3))):
                    if n:
                        ahead(2)
                    if h >= 1 or not isinstance(b, int) or b >= 1:
                        pe.wait_ge(exp_done, 3 * (NH * b + h - 1) + n + 1)
                    at = 0
                    for kt in kts:
                        w = S - kt * P
                        nc.tensor.matmul(sc[n][:, at:at + w], KS[par][:, h, kt * P:(kt + 1) * P], QS[par][:, h, kt * P:S],
                                         start=True, stop=False)
                        last = nc.tensor.matmul(sc[n][:, at:at + P], ident_b, mask_t, start=False, stop=True)
                        at += w
                    last.then_inc(sc_psum, 1)

            def weigh(b, par, h, ahead):
                pe.wait_ge(exp_done, 3 * (NH * b + h + 1))
                if h % 4 == 0 and (h or not isinstance(b, int) or b >= 1):
                    pe.wait_ge(oT_evac, NH // 4 * b + h // 4)
                r = slice(HG * (h % 4), HG * (h % 4) + HG)
                for kt in range(QT):
                    if kt == 1:
                        ahead(1)
                    last = nc.tensor.matmul(O[r, kt * P:S], V[par][:, kt, h, :], probs[h % 2][:, KOFF[kt]:KOFF[kt] + S - kt * P],
                                            start=kt == 0, stop=kt == QT - 1, skip_group_check=True)
                last.then_inc(pv_done, 1)

            def turn_heads(b, g, more):
                pe.wait_ge(oT_evac, NH // 4 * b + g + 1)
                if g == 0:
                    if isinstance(b, int) and b == 0:
                        pe.wait_ge(v_evac, 4)
                    else:
                        pe.wait_ge(way.placed, b)
                elif g >= 2:
                    pe.wait_ge(o_read, NH // 4 * b + g - 1)
                    if more:
                        pe.wait_ge(qk_evac, 4 * (b + 2) + 4)
                for i in range(QT):
                    last = nc.tensor.transpose(misc[g % 2][:, i * P:(i + 1) * P], oT[:, i * P:(i + 1) * P], ident)
                last.then_inc(o_turned, 1)

            def attend(b, par, nxt, more):
                pe.wait_ge(m_stacked, 16 * SPLITS * (b + 1))
                for h in range(NH):
                    if nxt and h == FIRST_SLOT:
                        pe.wait_ge(stacked, 16 * 12 * (b + 2))
                    todo = list(unit_range(h)) if nxt else []

                    def ahead(n):
                        for u in todo[:n]:
                            unit(b + 1, 1 - par, u)
                        del todo[:n]

                    scores(b, par, h, ahead)
                    ahead(2)
                    if h:
                        weigh(b, par, h - 1, ahead)
                    ahead(8)
                    if more and h == XT_SLOT:
                        turn_tokens(b + 2)
                    if more and h == Q_SLOT:
                        queries_keys(b + 2, range(2))
                    if more and h == K_SLOT:
                        queries_keys(b + 2, range(2, 4))
                    if not isinstance(b, int) or b >= 1:
                        if h == 1:
                            if nxt:
                                pe.wait_ge(v_evac, 2 * (b + 2))
                            else:
                                pe.wait_ge(wo_evac, 2 * b)
                            way.turn(pe, b - 1, 1 - par)
                        if h == 2:
                            way.logits(pe, b - 1)
                        if h == 4:
                            way.count(pe, b - 1)
                    if h % 4 == 1 and h > 1:
                        turn_heads(b, h // 4 - 1, more)
                    if nxt and h == MAXIMA_SLOT:
                        turn_maxima(b + 1)
                weigh(b, par, NH - 1, ahead)
                turn_heads(b, NH // 4 - 1, more)
                pe.wait_ge(o_read, NH // 4 * (b + 1))
                if nxt:
                    pe.wait_ge(mT_evac, b + 2)
                for c in range(HC):
                    for i in range(QT):
                        last = nc.tensor.transpose(misc[1 - c][:, i * P:(i + 1) * P], attn[:, i, c * P:(c + 1) * P], ident)
                    last.then_inc(aT_psum, 1)
                pe.wait_ge(aT_evac, HC * (b + 1))
                for n in range(2):
                    for i in range(2):
                        for c in range(HC):
                            t = 2 * n + i
                            last = nc.tensor.matmul(misc[1 - n][:, i * H:(i + 1) * H], attnT[:, c, t * P:(t + 1) * P],
                                                    wqkvo[:, 3, c, :], start=c == 0, stop=c == HC - 1)
                    last.then_inc(wo_psum, 1)
                if more:
                    values(b + 2, par)

            pe.wait_ge(w_in, 16 * NW)
            pe.wait_ge(ones_set, 6)
            pe.wait_ge(way.router_in, 16)
            schedule(pe, norm, project, values, maxima, attend)
            pe.wait_ge(wo_evac, 2 * B)
            way.turn(pe, B - 1, (B - 1) % 2)
            way.logits(pe, B - 1)
            way.count(pe, B - 1)
    return used + way.used


def normalize_on_act(nc, act, to, x, b, mv, rstd, minus, shift, step, count):
    nc.scalar.activation(minus[:, :], rstd[:, :], ACT.Identity, scale=-1.0).then_inc(step, 1)
    act.wait_ge(step, 2 * count + 1)
    for i in range(QT):
        last = nc.scalar.activation(shift[:, i:i + 1], mv[:, i, 0:1], ACT.Identity, scale=minus[:, i:i + 1])
    last.then_inc(step, 1)
    act.wait_ge(step, 2 * count + 2)
    for i in range(QT):
        last = nc.scalar.activation(to[:, i, :], x[:, QT * b + i, :], ACT.Identity, scale=rstd[:, i:i + 1],
                                    bias=shift[:, i:i + 1])
    return last


class Router:

    CHOOSE, PLACE = 12, 9

    def __init__(self, nc, keep_sems, keep, tag, x, cf, eps, zero, xs, scattered):
        def sb(name, shape, dt=F32):
            return keep.enter_context(nc.sbuf_tensor(f"{tag}_{name}", shape, dt))

        self.tag, self.zero, self.scattered = tag, zero, scattered
        self.router = sb("router", [P, HC, E])
        self.slots = [sb(f"slots{c}", [P, NT], I32) for c in range(2)]
        self.weights = [sb(f"weights{c}", [P, NT]) for c in range(2)]
        self.tile_expert = sb("tile_expert", [P, MTILES], I32)
        self.tile_row = sb("tile_row", [P, MTILES], I32)
        self.free = sb("free", [P, E])
        self.slotr = sb("slotr", [P, 2, NT])
        self.gap = sb("gap", [P, NT])
        self.router_in, self.step_end, self.pads_ready, self.pads_in, self.gap_ready, self.ratio_ready = (
            keep_sems.enter_context(nc.semaphore(f"{tag}_{name}"))
            for name in ("router_in", "step_end", "pads_ready", "pads_in", "gap_ready", "ratio_ready"))
        self.nc, self.x, self.eps, self.xs = nc, x, eps, xs
        self.ident = cf[:, CF_ID:CF_ID + P]
        self.earlier = cf[:, CF_TRI:CF_TRI + P]
        self.ones = cf[:, CF_ONE:CF_ONE + P]
        self.iota = cf[:, CF_IOTA:CF_IOTA + QT * E].rearrange("p (t e) -> p t e", e=E)
        self.fresh = cf[:, CF_FRESH:CF_FRESH + QT * E]
        self.region = cf[:, CF_REGION:CF_REGION + E]
        self.part = cf[:, CF_PART:CF_PART + 1]
        self.tiles = cf[:, CF_TB:CF_TB + MTILES * E].rearrange("p (t e) -> p t e", e=E)

    def begin(self, sems, ctx, turn_banks, logit_bank, xT=None):
        nc = self.nc

        def sb(name, shape, dt=F32):
            return ctx.enter_context(nc.sbuf_tensor(f"{self.tag}_{name}", shape, dt))

        def sem(name):
            self.used.append(sems.enter_context(nc.semaphore(f"{self.tag}_{name}")))
            return self.used[-1]

        self.used = []
        self.turn_banks, self.logit_bank = turn_banks, logit_bank
        self.stats_ = sb("stats", [P, QT, 6])
        self.mv = sb("mv", [P, QT, 2])
        self.lnvar = sb("lnvar", [P, QT])
        self.rstd = sb("rstd", [P, QT])
        self.pause = sb("pause", [P, 1])
        self.minus = sb("minus", [P, QT])
        self.shift = sb("shift", [P, QT])
        self.xh = [sb(f"xh{i}", [P, QT, H]) for i in range(2)]
        self.xT = sb("xT", [P, HC, S]) if xT is None else xT
        self.lg = sb("lg", [P, QT, E])
        self.top = [sb(f"top{c}", [P, QT]) for c in range(2)]
        self.hot = [sb(f"hot{c}", [P, QT, E]) for c in range(2)]
        self.tmp = sb("tmp", [P, QT, E])
        self.pick = sb("pick", [P, QT])
        self.both = sb("both", [P, QT, E])
        self.total = sb("total", [P, E, QT])
        self.run = sb("run", [P, E, QT])
        self.place_ = sb("place", [P, QT, E])
        self.slotf = sb("slotf", [P, 2, QT])
        self.slot_now = [sb(f"slot_now{i}", [P, 2, QT], I32) for i in range(2)]
        self.tick = sb("tick", [P, 2])

        self.stat_done = sem("stat_done")
        self.var_ready = sem("var_ready")
        self.ln_done = sem("ln_done")
        self.rstd_ready = sem("rstd_ready")
        self.xh_ready = sem("xh_ready")
        self.shift_step = sem("shift_step")
        self.turned = sem("turned")
        self.xT_ready = sem("xT_ready")
        self.routed = sem("routed")
        self.step = sem("step")
        self.both_ready = sem("both_ready")
        self.counted = sem("counted")
        self.placed = sem("placed")
        self.slot_ready = sem("slot_ready")
        self.xh_free = sem("xh_free")

    def end(self, ctx):
        nc = self.nc

        def sb(name, shape, dt=F32):
            return ctx.enter_context(nc.sbuf_tensor(f"{self.tag}_{name}", shape, dt))

        self.gap1 = sb("gap1", [P, NT])
        self.padded = sb("padded", [P, E])
        self.ends = sb("ends", [P, E])
        self.delta = sb("delta", [P, E])
        self.padf = sb("padf", [P, E])
        self.pads = sb("pads", [P, E], I32)
        self.tcmp = sb("tcmp", [P, MTILES, E])
        self.tsum = sb("tsum", [P, MTILES])
        self.cmp = sb("cmp", [P, 2, NT, E - 1])
        self.less = sb("less", [P, 2, NT])

    def start_dve(self, dve):
        nc = self.nc
        nc.vector.tensor_copy(self.free[:, :], self.region).then_inc(self.step_end, 1)
        dve.wait_ge(self.step_end, 1)

    def stats(self, dve, r):
        nc = self.nc
        for i in range(QT):
            last = nc.vector.bn_stats(self.stats_[:, i, :], self.x[:, QT * r + i, :])
        last.then_inc(self.stat_done, 1)
        dve.wait_ge(self.stat_done, r + 1)
        nc.vector.memset(self.pause[:, :], 0.0)
        for i in range(QT):
            last = nc.vector.bn_aggr(self.mv[:, i, :], self.stats_[:, i, :])
        last.then_inc(self.var_ready, 1)

    def normalize(self, dve, r, par):
        nc = self.nc
        dve.wait_ge(self.rstd_ready, r + 1)
        dve.wait_ge(self.xh_free, r + 1)
        for i in range(QT):
            last = nc.vector.tensor_scalar(self.xh[par][:, i, :], self.x[:, QT * r + i, :], self.mv[:, i, 0:1],
                                           self.rstd[:, i:i + 1], ALU.subtract, ALU.mult)
        last.then_inc(self.xh_ready, 1)

    def _then(self, dve, ins, r, k):
        ins.then_inc(self.step, 1)
        dve.wait_ge(self.step, (self.CHOOSE + self.PLACE) * r + k + 1)

    def choose(self, dve, r):
        nc = self.nc
        k = 0

        def then(ins):
            nonlocal k
            self._then(dve, ins, r, k)
            k += 1

        def over_e(a):
            return a.rearrange("p (t a) -> p t a", a=1).to_broadcast([P, QT, E])

        dve.wait_ge(self.routed, r + 1)
        then(nc.vector.tensor_copy(self.lg[:, :, :], self.logit_bank[:, 0:QT * E].rearrange("p (t e) -> p t e", e=E)))
        for c in range(2):
            then(nc.vector.tensor_reduce(self.top[c][:, :], self.lg[:, :, :], AX.X, ALU.max))
            then(nc.vector.tensor_tensor(self.tmp[:, :, :], self.lg[:, :, :], over_e(self.top[c][:, :]), ALU.is_equal))
            then(nc.vector.tensor_tensor(self.tmp[:, :, :], self.tmp[:, :, :], self.iota, ALU.mult))
            then(nc.vector.tensor_reduce(self.pick[:, :], self.tmp[:, :, :], AX.X, ALU.min))
            then(nc.vector.tensor_tensor(self.hot[c][:, :, :], self.iota, over_e(self.pick[:, :]), ALU.is_equal))
            if c == 0:
                then(nc.vector.scalar_tensor_tensor(out=self.lg[:, :, :], in0=self.hot[0][:, :, :], scalar=-BIG,
                                                    in1=self.lg[:, :, :], op0=ALU.mult, op1=ALU.add))
        assert k == self.CHOOSE
        nc.vector.tensor_tensor(self.both[:, :, :], self.hot[0][:, :, :], self.hot[1][:, :, :], ALU.add).then_inc(self.both_ready, 1)
        nc.vector.tensor_tensor(self.gap[:, bass.ds(QT * r, QT)], self.top[1][:, :], self.top[0][:, :],
                                ALU.subtract).then_inc(self.gap_ready, 1)

    def place(self, dve, r, par):
        nc = self.nc
        k = self.CHOOSE

        def then(ins):
            nonlocal k
            self._then(dve, ins, r, k)
            k += 1

        flat = "p e t -> p (e t)"
        dve.wait_ge(self.counted, r + 1)
        then(nc.vector.tensor_copy(self.total[:, :, :], self.logit_bank[:, 256:256 + QT * E].rearrange("p (t e) -> p e t", e=E)))
        then(nc.vector.tensor_tensor_scan(self.run[:, :, :].rearrange(flat), self.fresh, self.total[:, :, :].rearrange(flat), 0.0,
                                          ALU.mult, ALU.add))
        then(nc.vector.tensor_tensor(self.run[:, :, :], self.run[:, :, :],
                                     self.free[:, :].rearrange("p (e a) -> p e a", a=1).to_broadcast([P, E, QT]), ALU.add))
        then(nc.vector.tensor_copy(self.free[:, :], self.run[:, :, QT - 1]))
        then(nc.vector.tensor_tensor(self.run[:, :, :], self.run[:, :, :], self.total[:, :, :], ALU.subtract))
        ins = nc.vector.tensor_tensor(self.place_[:, :, :], self.logit_bank[:, 128:128 + QT * E].rearrange("p (t e) -> p t e", e=E),
                                      self.run[:, :, :].rearrange("p e t -> p t e"), ALU.add)
        ins.then_inc(self.placed, 1)
        dve.wait_ge(self.placed, r + 1)
        for c in range(2):
            then(nc.vector.tensor_tensor(self.tmp[:, :, :], self.hot[c][:, :, :], self.place_[:, :, :], ALU.mult))
            then(nc.vector.tensor_reduce(self.slotf[:, c, :], self.tmp[:, :, :], AX.X, ALU.add))
        assert k == self.CHOOSE + self.PLACE
        nc.vector.tensor_copy(self.slot_now[par][:, :, :], self.slotf[:, :, :]).then_inc(self.slot_ready, 1)
        for c in range(2):
            nc.vector.tensor_scalar(self.slotr[:, c, bass.ds(QT * r, QT)], self.slotf[:, c, :], 0.0, None, ALU.add)

    def finish_dve(self, dve):
        nc = self.nc
        done = 1

        def then(ins):
            nonlocal done
            done += 1
            ins.then_inc(self.step_end, 1)
            dve.wait_ge(self.step_end, done)

        then(nc.vector.tensor_tensor(self.padf[:, :], self.free[:, :], self.part.to_broadcast([P, E]), ALU.add))
        nc.vector.tensor_copy(self.pads[:, :], self.padf[:, :]).then_inc(self.pads_ready, 1)
        then(nc.vector.tensor_tensor(self.padded[:, :], self.free[:, :], self.region, ALU.subtract))
        then(nc.vector.tensor_scalar(self.padded[:, :], self.padded[:, :], 1.0 / P, (P - 1) / (2.0 * P), ALU.mult, ALU.add))
        then(nc.vector.tensor_scalar(self.padded[:, :], self.padded[:, :], MAGIC, MAGIC, ALU.add, ALU.subtract))
        then(nc.vector.tensor_scalar(self.padded[:, :], self.padded[:, :], float(P), None, ALU.mult))
        then(nc.vector.tensor_tensor_scan(self.ends[:, :], self.ones[:, 0:E], self.padded[:, :], 0.0, ALU.mult, ALU.add))
        then(nc.vector.tensor_tensor(self.tcmp[:, :, :], self.tiles,
                                     self.ends[:, :].rearrange("p (a e) -> p a e", a=1).to_broadcast([P, MTILES, E]), ALU.is_ge))
        then(nc.vector.tensor_reduce(self.tsum[:, :], self.tcmp[:, :, :], AX.X, ALU.add))
        then(nc.vector.tensor_scalar(self.tile_expert[:, :], self.tsum[:, :], float(E - 1), None, ALU.min))
        then(nc.vector.tensor_scalar(self.delta[:, :], self.padded[:, :], -1.0, float(CAP), ALU.mult, ALU.add))
        shape = [P, 2, NT, E - 1]
        then(nc.vector.tensor_tensor(self.cmp[:, :, :, :], self.slotr[:, :, :].rearrange("p c (t a) -> p c t a", a=1).to_broadcast(shape),
                                     self.region[:, 1:E].rearrange("p (a b e) -> p a b e", a=1, b=1).to_broadcast(shape), ALU.is_ge))
        then(nc.vector.tensor_tensor(self.cmp[:, :, :, :], self.cmp[:, :, :, :],
                                     self.delta[:, 0:E - 1].rearrange("p (a b e) -> p a b e", a=1, b=1).to_broadcast(shape), ALU.mult))
        then(nc.vector.tensor_reduce(self.less[:, :, :], self.cmp[:, :, :, :], AX.X, ALU.add))
        for c in range(2):
            then(nc.vector.tensor_tensor(self.slots[c][:, :], self.slotr[:, c, :], self.less[:, c, :], ALU.subtract))
        then(nc.vector.scalar_tensor_tensor(out=self.delta[:, E - 1:E], in0=self.ends[:, E - 1:E], scalar=-float(ROUTED),
                                            in1=self.delta[:, E - 1:E], op0=ALU.add, op1=ALU.add))
        then(nc.vector.tensor_tensor(self.tcmp[:, :, :], self.tcmp[:, :, :],
                                     self.delta[:, :].rearrange("p (a e) -> p a e", a=1).to_broadcast([P, MTILES, E]), ALU.mult))
        then(nc.vector.tensor_reduce(self.tsum[:, :], self.tcmp[:, :, :], AX.X, ALU.add))
        then(nc.vector.tensor_tensor(self.tile_row[:, :], self.tsum[:, :], self.tiles[:, :, 0], ALU.add))
        dve.wait_ge(self.ratio_ready, 1)
        then(nc.vector.tensor_scalar(self.gap1[:, :], self.gap[:, :], 1.0, None, ALU.add))
        then(nc.vector.reciprocal(self.weights[0][:, :], self.gap1[:, :]))
        then(nc.vector.tensor_tensor(self.weights[1][:, :], self.gap[:, :], self.weights[0][:, :], ALU.mult))

    def inv_std(self, act, r):
        nc = self.nc
        act.wait_ge(self.var_ready, r + 1)
        nc.scalar.activation(self.lnvar[:, :], self.mv[:, :, 1], ACT.Ln, bias=self.eps[:, 0:1]).then_inc(self.ln_done, 1)
        act.wait_ge(self.ln_done, r + 1)
        nc.scalar.activation(self.rstd[:, :], self.lnvar[:, :], ACT.Exp, scale=-0.5).then_inc(self.rstd_ready, 1)

    def normalize_by_act(self, act, r, par):
        act.wait_ge(self.rstd_ready, r + 1)
        act.wait_ge(self.xh_free, r + 1)
        normalize_on_act(self.nc, act, self.xh[par], self.x, r, self.mv, self.rstd, self.minus, self.shift,
                         self.shift_step, r).then_inc(self.xh_ready, 1)

    def turned_out(self, act, r):
        for c in range(HC):
            act.wait_ge(self.turned, HC * r + c + 1)
            self.nc.scalar.copy(self.xT[:, c, :], self.turn_banks[c][:, :]).then_inc(self.xT_ready, 1)

    def finish_act(self, act):
        act.wait_ge(self.gap_ready, B)
        self.nc.scalar.activation(self.gap[:, :], self.gap[:, :], ACT.Exp).then_inc(self.ratio_ready, 1)

    def turn(self, pe, r, par):
        pe.wait_ge(self.xh_ready, r + 1)
        for c in range(HC):
            for i in range(QT):
                last = self.nc.tensor.transpose(self.turn_banks[c][:, i * P:(i + 1) * P], self.xh[par][:, i, c * P:(c + 1) * P],
                                                self.ident)
            last.then_inc(self.turned, 1)

    def logits(self, pe, r):
        pe.wait_ge(self.xT_ready, HC * (r + 1))
        for i in range(QT):
            for c in range(HC):
                last = self.nc.tensor.matmul(self.logit_bank[:, i * E:(i + 1) * E], self.xT[:, c, i * P:(i + 1) * P],
                                             self.router[:, c, :], start=c == 0, stop=c == HC - 1)
        last.then_inc(self.routed, 1)

    def count(self, pe, r):
        pe.wait_ge(self.both_ready, r + 1)
        b = self.both[:, :, :].rearrange("p t e -> p (t e)")
        self.nc.tensor.matmul(self.logit_bank[:, 128:128 + QT * E], self.earlier, b, start=True, stop=True)
        self.nc.tensor.matmul(self.logit_bank[:, 256:256 + QT * E], self.ones, b, start=True, stop=True).then_inc(self.counted, 1)

    def _tick(self, n):
        return self.nc.gpsimd.tensor_tensor(self.tick[:, n:n + 1], self.part, self.part, ALU.mult)

    def start_pool(self, pool):
        for i in range(2):
            self._tick(1).then_inc(self.xh_free, 1)
            pool.wait_ge(self.xh_free, i + 1)

    def scatter(self, pool, r, par):
        pool.wait_ge(self.slot_ready, r + 1)
        self._tick(0)
        for c in range(2):
            for i in range(QT):
                pool.indirect_dma_start(out=self.xs, out_offset=bass.IndirectOffsetOnAxis(ap=self.slot_now[par][:, c, i:i + 1], axis=0),
                                        in_=self.xh[par][:, i, :], in_offset=None).then_inc(self.scattered, 16)
        pool.wait_ge(self.scattered, 16 * 2 * QT * (r + 1))
        self._tick(1).then_inc(self.xh_free, 1)
        pool.wait_ge(self.xh_free, r + 3)

    def finish_sp(self, sp):
        sp.wait_ge(self.pads_ready, 1)
        for e in range(E):
            row = sp.value_load(self.pads[0:1, e:e + 1], min_val=0, max_val=E * CAP - P)
            sp.dma_start(self.xs[bass.ds(row, P), :], self.zero[:, 0, :]).then_inc(self.pads_in, 16)
        sp.wait_ge(self.pads_in, 16 * E)


def build_experts(nc, sems, tag, cf, weights, weights_in, w_in, xs, ys, tile_expert, tile_row, stored):
    ident = cf[:, CF_ID:CF_ID + P]
    w1, w3, w2 = weights
    with ExitStack() as ctx:
        def sb(name, shape, dt=F32):
            return ctx.enter_context(nc.sbuf_tensor(f"{tag}_{name}", shape, dt))

        def ps(name, shape):
            return ctx.enter_context(nc.psum_tensor(f"{tag}_{name}", shape, F32))

        def sem(name):
            return sems.enter_context(nc.semaphore(f"{tag}_{name}"))

        xin = sb("xin", [P, LB, H])
        xT = [sb(f"exT{i}", [P, HC, P]) for i in range(2)]
        gate = [sb(f"gate{i}", [P, F]) for i in range(2)]
        hid = [sb(f"hid{i}", [P, F]) for i in range(2)]
        hT = [sb(f"hT{i}", [P, FC, P]) for i in range(2)]
        yo = sb("yo", [P, LB, H])
        xT_p = ps("xT_p", [P, 512])
        gate_p = [ps(f"gate_p{i}", [P, F]) for i in range(2)]
        up_p = [ps(f"up_p{i}", [P, F]) for i in range(2)]
        hT_p = ps("hT_p", [P, FC, P])
        out_p = [ps(f"out_p{i}", [P, 512]) for i in range(2)]

        loaded = [sem(f"loaded{i}") for i in range(LB)]
        x_turned = sem("ex_x_turned")
        xT_ready = sem("ex_xT_ready")
        gate_done = sem("ex_gate_done")
        up_done = sem("ex_up_done")
        silu_done = sem("ex_silu_done")
        hid_ready = sem("ex_hid_ready")
        h_turned = sem("ex_h_turned")
        hT_ready = sem("ex_hT_ready")
        out_done = sem("ex_out_done")
        y_ready = sem("ex_y_ready")

        ys_t = ys.rearrange("(t p) h -> t p h", p=P)

        def rows_of(eng, m, t):
            row = eng.value_load(tile_row[0:1, bass.ds(t, 1)], min_val=0, max_val=ROWS - P)
            return m[bass.ds(row, P), :]

        block = ctx.enter_context(nc.Block())

        @block.sync
        def _(sp):
            for e in range(1, E):
                sp.wait_ge(w_in, 48 * e)
                for w, w_dram in zip(weights, weights_in):
                    sp.dma_start(w[:, e], w_dram[e].rearrange("(c p) f -> p c f", p=P)).then_inc(w_in, 16)

        @block.gpsimd
        def _(pool):
            for n in range(LB):
                pool.dma_start(xin[:, n, :], rows_of(pool, xs, n)).then_inc(loaded[n], 16)
            with pool.Fori(0, MTILES // LB - 1) as it:
                for n in range(LB):
                    pool.wait_ge(x_turned, LB * it + n + 1)
                    pool.dma_start(xin[:, n, :], rows_of(pool, xs, LB * it + n + LB)).then_inc(loaded[n], 16)
                    pool.wait_ge(y_ready, LB * it + n + 1)
                    pool.dma_start(ys_t[LB * it + n], yo[:, n, :]).then_inc(stored[n], 16)
            for n in range(LB):
                t = MTILES - LB + n
                pool.wait_ge(y_ready, t + 1)
                pool.dma_start(ys_t[t], yo[:, n, :]).then_inc(stored[n], 16)
            for n in range(LB):
                pool.wait_ge(stored[n], 16 * (MTILES // LB))

        @block.scalar
        def _(act):
            nc.scalar.preload_act_table(ACT.Silu)

            def copy_x(t, par):
                act.wait_ge(x_turned, t + 1)
                nc.scalar.copy(xT[par][:, :, :], xT_p[:, 0:HC * P].rearrange("p (c t) -> p c t", c=HC)).then_inc(xT_ready, 1)

            def tile(t, par, more=True):
                act.wait_ge(gate_done, t + 1)
                nc.scalar.activation(gate[par][:, :], gate_p[par][:, :], ACT.Silu).then_inc(silu_done, 1)
                if more:
                    copy_x(t + 1, 1 - par)
                act.wait_ge(h_turned, t + 1)
                nc.scalar.copy(hT[par][:, :, :], hT_p[:, :, :]).then_inc(hT_ready, 1)

            copy_x(0, 0)
            with act.Fori(0, MTILES // 2 - 1) as it:
                for par in range(2):
                    tile(2 * it + par, par)
            tile(MTILES - 2, 0)
            tile(MTILES - 1, 1, more=False)

        @block.vector
        def _(dve):
            def put_out(it, t, par, n):
                dve.wait_ge(out_done, t + 1)
                nc.vector.tensor_copy(yo[:, n, :], out_p[par][:, 0:H]).then_inc(y_ready, 1)

            def gated(t, par):
                dve.wait_ge(up_done, t + 1)
                dve.wait_ge(silu_done, t + 1)
                nc.vector.tensor_tensor(hid[par][:, :], gate[par][:, :], up_p[par][:, :], ALU.mult).then_inc(hid_ready, 1)

            gated(0, 0)
            for n in range(1, LB):
                gated(n, n % 2)
                put_out(0, n - 1, (n - 1) % 2, n - 1)

            def round_(it):
                for n in range(LB):
                    gated(LB * it + n, n % 2)
                    m = (n - 1) % LB
                    if n:
                        dve.wait_ge(stored[m], 16 * it)
                    elif not isinstance(it, int):
                        dve.wait_ge(stored[m], 16 * (it - 1))
                    put_out(it, LB * it + n - 1, m % 2, m)

            round_(1)
            with dve.Fori(2, MTILES // LB) as it:
                round_(it)
            dve.wait_ge(stored[LB - 1], 16 * (MTILES // LB - 1))
            put_out(0, MTILES - 1, (MTILES - 1) % 2, LB - 1)

        @block.tensor
        def _(pe):
            def turn_x(t, par, n, round_):
                pe.wait_ge(loaded[n], 16 * (round_ + 1))
                if not isinstance(t, int) or t >= 1:
                    pe.wait_ge(xT_ready, t)
                for c in range(HC):
                    last = nc.tensor.transpose(xT_p[:, c * P:(c + 1) * P], xin[:, n, c * P:(c + 1) * P], ident)
                last.then_inc(x_turned, 1)

            def gate_up(t, par):
                e = nc.tensor.value_load(tile_expert[0:1, bass.ds(t, 1)], min_val=0, max_val=E - 1)
                pe.wait_ge(w_in, 48 * e + 48)
                pe.wait_ge(xT_ready, t + 1)
                if not isinstance(t, int) or t >= 2:
                    pe.wait_ge(silu_done, t - 1)
                for c in range(HC):
                    last = nc.tensor.matmul(gate_p[par][:, :], xT[par][:, c, :], w1[:, e, c, :], start=c == 0, stop=c == HC - 1)
                last.then_inc(gate_done, 1)
                if not isinstance(t, int) or t >= 2:
                    pe.wait_ge(hid_ready, t - 1)
                for c in range(HC):
                    last = nc.tensor.matmul(up_p[par][:, :], xT[par][:, c, :], w3[:, e, c, :], start=c == 0, stop=c == HC - 1)
                last.then_inc(up_done, 1)
                return e

            def turn_h(t, par):
                pe.wait_ge(hid_ready, t + 1)
                if not isinstance(t, int) or t >= 1:
                    pe.wait_ge(hT_ready, t)
                for c in range(FC):
                    last = nc.tensor.transpose(hT_p[:, c, :], hid[par][:, c * P:(c + 1) * P], ident)
                last.then_inc(h_turned, 1)

            def down(t, par):
                e = nc.tensor.value_load(tile_expert[0:1, bass.ds(t, 1)], min_val=0, max_val=E - 1)
                pe.wait_ge(hT_ready, t + 1)
                if not isinstance(t, int) or t >= 2:
                    pe.wait_ge(y_ready, t - 1)
                for c in range(FC):
                    last = nc.tensor.matmul(out_p[par][:, 0:H], hT[par][:, c, :], w2[:, e, c, :], start=c == 0, stop=c == FC - 1)
                last.then_inc(out_done, 1)

            turn_x(0, 0, 0, 0)
            gate_up(0, 0)
            turn_x(1, 1, 1, 0)

            def round_(it):
                for n in range(LB):
                    t = LB * it + n
                    turn_h(t, n % 2)
                    gate_up(t + 1, (n + 1) % 2)
                    turn_x(t + 2, n % 2, (n + 2) % LB, it + (n + 2) // LB)
                    down(t, n % 2)

            round_(0)
            with pe.Fori(1, MTILES // LB - 1) as it:
                round_(it)
            for t in range(MTILES - LB, MTILES):
                turn_h(t, t % 2)
                if t + 1 < MTILES:
                    gate_up(t + 1, (t + 1) % 2)
                if t + 2 < MTILES:
                    turn_x(t + 2, t % 2, (t + 2) % LB, (t + 2) // LB)
                down(t, t % 2)


class Gather:

    def __init__(self, nc, sems, ctx, tag, x, ys, way, fetched):
        self.nc, self.x, self.ys, self.way, self.fetched = nc, x, ys, way, fetched
        self.got = ctx.enter_context(nc.sbuf_tensor(f"{tag}_got", [P, RB, 2, H], F32))
        self.first = sems.enter_context(nc.semaphore(f"{tag}_first"))
        self.added = sems.enter_context(nc.semaphore(f"{tag}_added"))

    def fetch(self, pool, tiles):
        for t in tiles:
            if t >= RB:
                pool.wait_ge(self.added, t - RB + 1)
            for c in range(2):
                pool.indirect_dma_start(out=self.got[:, t % RB, c, :], out_offset=None, in_=self.ys,
                                        in_offset=bass.IndirectOffsetOnAxis(ap=self.way.slots[c][:, t:t + 1], axis=0)
                                        ).then_inc(self.fetched[t % RB], 16)

    def settle(self, pool, tiles):
        for n in range(RB):
            pool.wait_ge(self.fetched[n], 32 * len(range(n, tiles, RB)))

    def add(self, dve, tiles):
        for t in tiles:
            dve.wait_ge(self.fetched[t % RB], 32 * (t // RB + 1))
            self.nc.vector.scalar_tensor_tensor(out=self.x[:, t, :], in0=self.got[:, t % RB, 0, :],
                                                scalar=self.way.weights[0][:, t:t + 1], in1=self.x[:, t, :],
                                                op0=ALU.mult, op1=ALU.add).then_inc(self.first, 1)
        for t in tiles:
            dve.wait_ge(self.first, t + 1)
            self.nc.vector.scalar_tensor_tensor(out=self.x[:, t, :], in0=self.got[:, t % RB, 1, :],
                                                scalar=self.way.weights[1][:, t:t + 1], in1=self.x[:, t, :],
                                                op0=ALU.mult, op1=ALU.add).then_inc(self.added, 1)


def build_combine(nc, sems, tag, x, ys, way, fetched, out):
    with ExitStack() as ctx:
        gather = Gather(nc, sems, ctx, tag, x, ys, way, fetched)
        written = sems.enter_context(nc.semaphore(f"{tag}_written"))
        block = ctx.enter_context(nc.Block())

        @block.gpsimd
        def _(pool):
            gather.fetch(pool, range(NT))

        @block.vector
        def _(dve):
            for t in range(NT):
                gather.add(dve, [t])

        @block.sync
        def _(sp):
            for t in range(0, NT, 2):
                sp.wait_ge(gather.added, t + 2)
                sp.dma_start(out[:, t:t + 2, :], x[:, t:t + 2, :]).then_inc(written, 16)
            sp.wait_ge(written, 16 * (NT // 2))


def build_mamba(nc, sems, x, cf, cb, d, eps, ys, way1, fetched, way2):
    ident = cf[:, CF_ID:CF_ID + P]
    AHEAD = 4
    ones = cf[:, CF_ONE:CF_ONE + 1].rearrange("p (a t) -> p a t", a=1).to_broadcast([P, HC, S])
    with ExitStack() as ctx:
        def sb(name, shape, dt=F32):
            return ctx.enter_context(nc.sbuf_tensor(f"ma_{name}", shape, dt))

        def ps(name, shape):
            return ctx.enter_context(nc.psum_tensor(f"ma_{name}", shape, F32))

        def sem(name):
            return sems.enter_context(nc.semaphore(f"ma_{name}"))

        convw = sb("convw", [P, HC, TAPS])
        convb = sb("convb", [P, HC])
        wdt = sb("wdt", [P, HC, RANK])
        wdt2 = sb("wdt2", [RANK, H])
        dtb = sb("dtb", [P, HC])
        wbc = sb("wbc", [P, HC, SPLITS * BCR])
        A = sb("A", [P, HC, NS])
        D = sb("D", [P, HC])
        taps = sb("taps", [P, HC, TAPS, P])
        stats = sb("stats", [P, QT, 6])
        mv = sb("mv", [P, QT, 2])
        lnvar = sb("lnvar", [P, QT])
        rstd = sb("rstd", [P, QT])
        pause = sb("pause", [P, 1])
        minus = sb("minus", [P, QT])
        shift = sb("shift", [P, QT])
        xh = sb("xh", [P, QT, H])
        xp = sb("xp", [P, HC, TAPS - 1 + S])
        xc = [sb(f"xc{i}", [P, HC, S]) for i in range(2)]
        low = sb("low", [RANK, S])
        mag = sb("mag", [P, HC, S])
        ez = sb("ez", [P, HC, S])
        up = sb("up", [P, HC, S])
        pos = sb("pos", [P, HC, S])
        dt = [sb(f"dt{i}", [P, HC, S]) for i in range(2)]
        dtx = [sb(f"dtx{i}", [P, HC, S]) for i in range(2)]
        bc32 = sb("bc32", [SPLITS * BCR, S])
        bcs = [sb(f"bcs{i}", [SPLITS * BCR, S], BF16) for i in range(2)]
        dA = [sb(f"dA{i}", [P, HC, S]) for i in range(AHEAD)]
        dBx = [sb(f"dBx{i}", [P, HC, S]) for i in range(2)]
        hs = [sb(f"hs{i}", [P, HC, S]) for i in range(2)]
        hC = [sb(f"hC{i}", [P, HC, S]) for i in range(2)]
        yT = sb("yT", [P, HC, S])

        bB = [ps(f"bB{i}", [P, 512]) for i in range(2)]
        bC = [ps(f"bC{i}", [P, 512]) for i in range(2)]
        yp = ps("yp", [P, HC, 512])
        pp = [ps(f"pp{i}", [P, 512]) for i in range(2)]

        w_in = sem("w_in")
        setup = sem("setup")
        a_exp = sem("a_exp")
        stat_done = sem("stat_done")
        var_ready = sem("var_ready")
        ln_done = sem("ln_done")
        rstd_ready = sem("rstd_ready")
        xh_ready = sem("xh_ready")
        shift_step = sem("shift_step")
        turned = sem("turned")
        xp_ready = sem("xp_ready")
        conv_done = sem("conv_done")
        xc_ready = sem("xc_ready")
        low_done = sem("low_done")
        low_ready = sem("low_ready")
        bc_done = sem("bc_done")
        bc_copied = sem("bc_copied")
        bc_rest1 = sem("bc_rest1")
        bc_part2 = sem("bc_part2")
        bc_ready = sem("bc_ready")
        z_done = sem("z_done")
        z_read = sem("z_read")
        exp_z = sem("exp_z")
        one_z = sem("one_z")
        soft_step = sem("soft_step")
        log_z = sem("log_z")
        dt_ready = sem("dt_ready")
        dtx_ready = sem("dtx_ready")
        spread_B = sem("spread_B")
        spread_C = sem("spread_C")
        dA_ready = sem("dA_ready")
        dBx_ready = sem("dBx_ready")
        scanned = sem("scanned")
        hC_ready = sem("hC_ready")
        summed = sem("summed")
        y_ready = sem("y_ready")
        y_turned = sem("y_turned")
        y_added = sem("y_added")
        NW = 8

        gather = Gather(nc, sems, ctx, "f1", x, ys, way1, fetched)
        way2.begin(sems, ctx, pp, pp[0])

        def schedule(eng, norm, prepare, start, states):
            for b in range(2):
                for n in sorted(norm):
                    norm[n](b, b)
                if b == 0:
                    for n in sorted(prepare):
                        prepare[n](0, 0)
            start()
            states(0, 0, True, True)
            with eng.Fori(0, (B - 4) // 2) as it:
                for par in range(2):
                    states(2 * it + 1 + par, 1 - par, True, True)
            states(B - 3, 1, True, True)
            states(B - 2, 0, True, False)
            states(B - 1, 1, False, False)

        def between(n, b, par, nxt, more, norm, prepare):
            if nxt and n in prepare:
                prepare[n](b + 1, 1 - par)
            if more and n in norm:
                norm[n](b + 2, par)

        block = ctx.enter_context(nc.Block())

        @block.sync
        def _(sp):
            by_half = "(c p) n -> p c n"
            sp.dma_start(convw[:, :, :], d["conv_w"].rearrange(by_half, p=P)).then_inc(w_in, 16)
            sp.dma_start(convb[:, :], d["conv_b"]).then_inc(w_in, 16)
            sp.dma_start(wdt[:, :, :], d["x_proj_dt_w"].rearrange(by_half, p=P)).then_inc(w_in, 16)
            sp.dma_start(wdt2[:, :], d["dt_proj_w"]).then_inc(w_in, 16)
            sp.dma_start(dtb[:, :], d["dt_proj_b"]).then_inc(w_in, 16)
            sp.dma_start(wbc[:, :, :], d["BC_proj_w"].rearrange(by_half, p=P)).then_inc(w_in, 16)
            sp.dma_start(A[:, :, :], d["A_log"].rearrange(by_half, p=P)).then_inc(w_in, 16)
            sp.dma_start(D[:, :], d["D_param"]).then_inc(w_in, 16)

        @block.gpsimd
        def _(pool):
            def soft(b, par):
                pool.wait_ge(log_z, b + 1)
                if not isinstance(b, int) or b >= 2:
                    pool.wait_ge(dA_ready, NS * (b - 1))
                    pool.wait_ge(dBx_ready, NS * (b - 1))
                nc.gpsimd.tensor_tensor(up[:, :, :], up[:, :, :], ones, ALU.subtract).then_inc(soft_step, 1)
                pool.wait_ge(soft_step, 3 * b + 1)
                nc.gpsimd.tensor_tensor(ez[:, :, :], ez[:, :, :], up[:, :, :], ALU.subtract).then_inc(soft_step, 1)
                pool.wait_ge(soft_step, 3 * b + 2)
                nc.gpsimd.tensor_tensor(mag[:, :, :], mag[:, :, :], ez[:, :, :], ALU.add).then_inc(soft_step, 1)
                pool.wait_ge(soft_step, 3 * b + 3)
                nc.gpsimd.tensor_tensor(dt[par][:, :, :], mag[:, :, :], pos[:, :, :], ALU.add).then_inc(dt_ready, 1)
                pool.wait_ge(dt_ready, b + 1)
                nc.gpsimd.tensor_tensor(dtx[par][:, :, :], dt[par][:, :, :], xc[par][:, :, :], ALU.mult).then_inc(dtx_ready, 1)

            def split(b, par):
                pool.wait_ge(bc_copied, b + 1)
                nc.gpsimd.tensor_tensor(bc32[:, :], bc32[:, :], bcs[par][:, :], ALU.subtract).then_inc(bc_rest1, 1)
                pool.wait_ge(bc_part2, b + 1)
                r = slice(2 * BCR, 3 * BCR)
                nc.gpsimd.tensor_tensor(bcs[par][r], bc32[r], bcs[par][r], ALU.subtract).then_inc(bc_ready, 1)
                pool.wait_ge(bc_ready, b + 1)

            prepare = {0: split, 1: soft}

            def states(b, par, nxt, more):
                for n in range(2):
                    between(n, b, par, nxt, more, {}, prepare)
                if not isinstance(b, int) or b >= 1:
                    way2.scatter(pool, b - 1, 1 - par)

            way2.start_pool(pool)
            gather.fetch(pool, range(2 * QT))
            gather.settle(pool, 2 * QT)

            def start():
                gather.fetch(pool, range(2 * QT, NT))
                gather.settle(pool, NT)

            schedule(pool, {}, prepare, start, states)
            way2.scatter(pool, B - 1, (B - 1) % 2)

        @block.scalar
        def _(act):
            nc.scalar.preload_act_table_set(LN_EXP)
            act.wait_ge(w_in, 16 * NW)
            nc.scalar.activation(A[:, :, :], A[:, :, :], ACT.Exp).then_inc(a_exp, 1)

            def inv_std(b, par):
                act.wait_ge(var_ready, b + 1)
                nc.scalar.activation(lnvar[:, :], mv[:, :, 1], ACT.Ln, bias=eps[:, 0:1]).then_inc(ln_done, 1)
                act.wait_ge(ln_done, b + 1)
                nc.scalar.activation(rstd[:, :], lnvar[:, :], ACT.Exp, scale=-0.5).then_inc(rstd_ready, 1)
                act.wait_ge(rstd_ready, b + 1)
                if not isinstance(b, int) or b >= 1:
                    act.wait_ge(turned, HC * b)
                normalize_on_act(nc, act, xh, x, b, mv, rstd, minus, shift, shift_step, b).then_inc(xh_ready, 1)

            def turn(b, par):
                for c in range(HC):
                    act.wait_ge(turned, HC * b + c + 1)
                    nc.scalar.copy(xp[:, c, TAPS - 1:], pp[c][:, :]).then_inc(xp_ready, 1)

            def conv(b, par):
                if not isinstance(b, int) or b >= 2:
                    act.wait_ge(y_ready, b - 1)
                    act.wait_ge(dtx_ready, b - 1)
                for c in range(HC):
                    act.wait_ge(conv_done, HC * b + c + 1)
                    nc.scalar.activation(xc[par][:, c, :], pp[c][:, :], ACT.Silu, bias=convb[:, c:c + 1]).then_inc(xc_ready, 1)
                nc.scalar.preload_act_table_set(LN_EXP)

            def low_rank(b, par):
                act.wait_ge(low_done, b + 1)
                nc.scalar.copy(low[:, :], pp[0][0:RANK, :]).then_inc(low_ready, 1)
                act.wait_ge(bc_done, b + 1)
                if not isinstance(b, int) or b >= 2:
                    act.wait_ge(spread_C, NS * (b - 1))
                if not isinstance(b, int) or b >= 1:
                    act.wait_ge(bc_ready, b)
                nc.scalar.copy(bcs[par][:, :], pp[1][0:SPLITS * BCR, :])
                nc.scalar.copy(bc32[:, :], pp[1][0:SPLITS * BCR, :]).then_inc(bc_copied, 1)

            def second_part(b, par):
                act.wait_ge(bc_rest1, b + 1)
                nc.scalar.copy(bcs[par][BCR:2 * BCR], bc32[BCR:2 * BCR])
                nc.scalar.copy(bcs[par][2 * BCR:3 * BCR], bc32[2 * BCR:3 * BCR]).then_inc(bc_part2, 1)

            def softplus(b, par):
                if not isinstance(b, int) or b >= 1:
                    act.wait_ge(dt_ready, b)
                for c in range(HC):
                    act.wait_ge(z_done, HC * b + c + 1)
                    nc.scalar.activation(mag[:, c, :], pp[c][:, :], ACT.Abs, bias=dtb[:, c:c + 1])
                    nc.scalar.activation(pos[:, c, :], pp[c][:, :], ACT.Relu, bias=dtb[:, c:c + 1]).then_inc(z_read, 1)
                act.wait_ge(z_read, HC * (b + 1))
                nc.scalar.activation(ez[:, :, :], mag[:, :, :], ACT.Exp, scale=-1.0).then_inc(exp_z, 1)
                act.wait_ge(exp_z, b + 1)
                nc.scalar.activation(up[:, :, :], ez[:, :, :], ACT.Identity, bias=1.0).then_inc(one_z, 1)
                act.wait_ge(one_z, b + 1)
                nc.scalar.activation(mag[:, :, :], up[:, :, :], ACT.Ln).then_inc(log_z, 1)

            norm = {14: inv_std}
            prepare = {4: turn, 7: conv, 9: low_rank, 10: second_part, 11: softplus}

            def states(b, par, nxt, more):
                act.wait_ge(dt_ready, b + 1)
                for n in range(NS):
                    g = NS * b + n
                    if n >= AHEAD or not isinstance(b, int) or b >= 1:
                        act.wait_ge(scanned, g - AHEAD + 1)
                    for c in range(HC):
                        last = nc.scalar.activation(dA[n % AHEAD][:, c, 1:], dt[par][:, c, 1:], ACT.Exp, scale=A[:, c, n:n + 1])
                    last.then_inc(dA_ready, 1)
                    between(n, b, par, nxt, more, norm, prepare)
                    if not isinstance(b, int) or b >= 1:
                        if n == 5:
                            way2.inv_std(act, b - 1)
                            way2.normalize_by_act(act, b - 1, 1 - par)
                        if n == 13:
                            way2.turned_out(act, b - 1)

            act.wait_ge(setup, 1)
            schedule(act, norm, prepare, lambda: None, states)
            way2.inv_std(act, B - 1)
            way2.normalize_by_act(act, B - 1, (B - 1) % 2)
            way2.turned_out(act, B - 1)

        @block.vector
        def _(dve):
            nc.vector.memset(xp[:, :, 0:TAPS - 1], 0.0)
            for i in range(AHEAD):
                nc.vector.memset(dA[i][:, :, 0:1], 0.0)
            dve.wait_ge(w_in, 16 * NW)
            for c in range(HC):
                for k in range(TAPS):
                    nc.vector.tensor_scalar(taps[:, c, k, :], ident, convw[:, c, k:k + 1], None, ALU.mult)
            dve.wait_ge(a_exp, 1)
            nc.vector.tensor_scalar(A[:, :, :], A[:, :, :], -1.0, None, ALU.mult).then_inc(setup, 1)

            def norm_stats(b, par):
                if isinstance(b, int) and b < 2:
                    gather.add(dve, range(QT * b, QT * b + QT))
                    dve.wait_ge(gather.added, QT * b + QT)
                    if b:
                        dve.wait_ge(xh_ready, b)
                if isinstance(b, int) and b == 2:
                    dve.wait_ge(gather.added, NT - 2)
                for i in range(QT):
                    last = nc.vector.bn_stats(stats[:, i, :], x[:, QT * b + i, :])
                last.then_inc(stat_done, 1)
                dve.wait_ge(stat_done, b + 1)
                nc.vector.memset(pause[:, :], 0.0)
                for i in range(QT):
                    last = nc.vector.bn_aggr(mv[:, i, :], stats[:, i, :])
                last.then_inc(var_ready, 1)

            norm = {11: norm_stats}

            def both(bank):
                return bank[:, :].rearrange("p (a t) -> p a t", a=1).to_broadcast([P, HC, S])

            def drive(b, par, n):
                g = NS * b + n
                if n == 0:
                    dve.wait_ge(dtx_ready, b + 1)
                dve.wait_ge(spread_B, g + 1)
                nc.vector.tensor_tensor(dBx[n % 2][:, :, :], dtx[par][:, :, :], both(bB[n % 2]), ALU.mult).then_inc(dBx_ready, 1)

            def scan(b, par, n):
                g = NS * b + n
                dve.wait_ge(dBx_ready, g + 1)
                dve.wait_ge(dA_ready, g + 1)
                flat = "p c t -> p (c t)"
                nc.vector.tensor_tensor_scan(hs[n % 2][:, :, :].rearrange(flat), dA[n % AHEAD][:, :, :].rearrange(flat),
                                             dBx[n % 2][:, :, :].rearrange(flat), 0.0, ALU.mult, ALU.add).then_inc(scanned, 1)

            def read(b, par, n):
                g = NS * b + n
                dve.wait_ge(scanned, g + 1)
                dve.wait_ge(spread_C, g + 1)
                if n >= 2 or not isinstance(b, int) or b >= 1:
                    dve.wait_ge(summed, g - 1)
                nc.vector.tensor_tensor(hC[n % 2][:, :, :], hs[n % 2][:, :, :], both(bC[n % 2]), ALU.mult).then_inc(hC_ready, 1)

            def start():
                drive(0, 0, 0)
                scan(0, 0, 0)

            def states(b, par, nxt, more):
                for n in range(NS):
                    if n < NS - 1:
                        drive(b, par, n + 1)
                    read(b, par, n)
                    if n < NS - 1:
                        scan(b, par, n + 1)
                    between(n, b, par, nxt, more, norm, {})
                    if isinstance(b, int) and b == 0:
                        if n < 12:
                            gather.add(dve, range(2 * QT + 2 * n, 2 * QT + 2 * n + 2))
                        else:
                            dve.wait_ge(gather.added, NT)
                    else:
                        if n == 3:
                            dve.wait_ge(y_added, HC * b)
                            nc.vector.memset(pause[:, :], 0.0)
                            way2.stats(dve, b - 1)
                        if n == 14:
                            way2.choose(dve, b - 1)
                        if n == 15:
                            way2.place(dve, b - 1, 1 - par)
                if nxt:
                    drive(b + 1, 1 - par, 0)
                dve.wait_ge(summed, NS * (b + 1))
                if not isinstance(b, int) or b >= 1:
                    dve.wait_ge(y_turned, HC * b)
                for c in range(HC):
                    last = nc.vector.scalar_tensor_tensor(out=yT[:, c, :], in0=xc[par][:, c, :], scalar=D[:, c:c + 1],
                                                          in1=yp[:, c, :], op0=ALU.mult, op1=ALU.add)
                last.then_inc(y_ready, 1)
                if nxt:
                    scan(b + 1, 1 - par, 0)
                for c in range(HC):
                    dve.wait_ge(y_turned, HC * b + c + 1)
                    xb = x[:, bass.ds(QT * b, QT), c * P:(c + 1) * P]
                    nc.vector.tensor_tensor(xb, xb, pp[c][:, :].rearrange("p (i e) -> p i e", i=QT), ALU.add).then_inc(y_added, 1)

            way2.start_dve(dve)
            schedule(dve, norm, {}, start, states)
            dve.wait_ge(y_added, HC * B)
            way2.stats(dve, B - 1)
            way2.choose(dve, B - 1)
            way2.place(dve, B - 1, (B - 1) % 2)

        @block.tensor
        def _(pe):
            def turn(b, par):
                pe.wait_ge(xh_ready, b + 1)
                if not isinstance(b, int) or b >= 2:
                    pe.wait_ge(y_added, HC * (b - 1))
                elif b == 1:
                    pe.wait_ge(z_read, HC)
                for c in range(HC):
                    for i in range(QT):
                        last = nc.tensor.transpose(pp[c][:, i * P:(i + 1) * P], xh[:, i, c * P:(c + 1) * P], ident)
                    last.then_inc(turned, 1)

            def conv(c):
                def step(b, par):
                    pe.wait_ge(xp_ready, HC * (b + 1))
                    for k in range(TAPS):
                        last = nc.tensor.matmul(pp[c][:, :], taps[:, c, k, :], xp[:, c, k:k + S], start=k == 0, stop=k == TAPS - 1)
                    last.then_inc(conv_done, 1)
                return step

            def low_rank(b, par):
                pe.wait_ge(xc_ready, HC * (b + 1))
                for c in range(HC):
                    last = nc.tensor.matmul(pp[0][0:RANK, :], wdt[:, c, :], xc[par][:, c, :], start=c == 0, stop=c == HC - 1)
                last.then_inc(low_done, 1)
                for c in range(HC):
                    last = nc.tensor.matmul(pp[1][0:SPLITS * BCR, :], wbc[:, c, :], xc[par][:, c, :], start=c == 0, stop=c == HC - 1)
                last.then_inc(bc_done, 1)

            def zed(b, par):
                pe.wait_ge(low_ready, b + 1)
                pe.wait_ge(bc_copied, b + 1)
                for c in range(HC):
                    nc.tensor.matmul(pp[c][:, :], wdt2[:, c * P:(c + 1) * P], low[:, :], start=True, stop=True).then_inc(z_done, 1)

            prepare = {1: turn, 4: conv(0), 5: conv(1), 7: low_rank, 9: zed}

            def spread_b(b, par, n):
                g = NS * b + n
                if n == 0:
                    pe.wait_ge(bc_ready, b + 1)
                if n >= 2 or not isinstance(b, int) or b >= 1:
                    pe.wait_ge(dBx_ready, g - 1)
                sel = cb[0:SPLITS * BCR, CB_SEL + n * P:CB_SEL + (n + 1) * P]
                nc.tensor.matmul(bB[n % 2][:, :], sel, bcs[par][:, :], start=True, stop=True).then_inc(spread_B, 1)

            def spread_c(b, par, n):
                g = NS * b + n
                if n >= 2 or not isinstance(b, int) or b >= 1:
                    pe.wait_ge(hC_ready, g - 1)
                sel = cb[0:SPLITS * BCR, CB_SEL + (NS + n) * P:CB_SEL + (NS + n + 1) * P]
                nc.tensor.matmul(bC[n % 2][:, :], sel, bcs[par][:, :], start=True, stop=True).then_inc(spread_C, 1)

            def add_up(b, par, n):
                g = NS * b + n
                pe.wait_ge(hC_ready, g + 1)
                if n == 0 and (not isinstance(b, int) or b >= 1):
                    pe.wait_ge(y_ready, b)
                for c in range(HC):
                    last = nc.tensor.matmul(yp[:, c, :], ident, hC[n % 2][:, c, :], start=n == 0, stop=n == NS - 1)
                last.then_inc(summed, 1)

            def states(b, par, nxt, more):
                for n in range(NS):
                    if n < NS - 2:
                        spread_b(b, par, n + 2)
                    elif nxt:
                        spread_b(b + 1, 1 - par, n + 2 - NS)
                    if n < NS - 1:
                        spread_c(b, par, n + 1)
                    elif nxt:
                        spread_c(b + 1, 1 - par, 0)
                    between(n, b, par, nxt, more, {}, prepare)
                    add_up(b, par, n)
                    if not isinstance(b, int) or b >= 1:
                        if n == 12:
                            if nxt:
                                pe.wait_ge(z_read, HC * (b + 2))
                            else:
                                pe.wait_ge(y_added, HC * b)
                            way2.turn(pe, b - 1, 1 - par)
                        if n == 13:
                            way2.logits(pe, b - 1)
                        if n == 14:
                            way2.count(pe, b - 1)
                pe.wait_ge(y_ready, b + 1)
                if isinstance(b, int) and b == 0:
                    pe.wait_ge(z_read, HC * (b + 2))
                else:
                    pe.wait_ge(way2.placed, b)
                for c in range(HC):
                    for i in range(QT):
                        last = nc.tensor.transpose(pp[c][:, i * P:(i + 1) * P], yT[:, c, i * P:(i + 1) * P], ident)
                    last.then_inc(y_turned, 1)

            pe.wait_ge(w_in, 16 * NW)
            pe.wait_ge(way2.router_in, 16)
            pe.wait_ge(setup, 1)
            def start():
                spread_b(0, 0, 0)
                spread_b(0, 0, 1)
                spread_c(0, 0, 0)

            schedule(pe, {}, prepare, start, states)
            pe.wait_ge(y_added, HC * B)
            way2.turn(pe, B - 1, (B - 1) % 2)
            way2.logits(pe, B - 1)
            way2.count(pe, B - 1)


def build_ffn(nc, sems, tag, cf, weights_in, xs, ys, way, stored):
    with ExitStack() as ctx:
        def sb(name, shape):
            return ctx.enter_context(nc.sbuf_tensor(f"{tag}_{name}", shape, F32))

        w1 = sb("w1", [P, E, HC, F])
        w3 = sb("w3", [P, E, HC, F])
        w2 = sb("w2", [P, E, FC, H])
        w_in = sems.enter_context(nc.semaphore(f"{tag}_w_in"))
        way.end(ctx)
        with nc.Block() as block:
            @block.vector
            def _(dve):
                way.finish_dve(dve)

            @block.scalar
            def _(act):
                nc.scalar.preload_act_table_set(LN_EXP)
                way.finish_act(act)

            @block.sync
            def _(sp):
                for w, w_dram in zip((w1, w3, w2), weights_in[1:]):
                    sp.dma_start(w[:, 0], w_dram[0].rearrange("(c p) f -> p c f", p=P)).then_inc(w_in, 16)
                way.finish_sp(sp)
        build_experts(nc, sems, tag, cf, (w1, w3, w2), weights_in[1:], w_in, xs, ys, way.tile_expert, way.tile_row, stored)


def build_layers(nc, hidden, cf_in, cb_in, attention_in, mamba_in, ffn_in, out):
    token_major = "(t p) h -> p t h"
    x_in = hidden.rearrange("b s h -> (b s) h").rearrange(token_major, p=P)
    x_out = out.rearrange("b s h -> (b s) h").rearrange(token_major, p=P)
    xs = nc.dram_tensor("expert_rows_in", [ROWS, H], F32).ap()
    ys = nc.dram_tensor("expert_rows_out", [MTILES * P, H], F32).ap()
    with ExitStack() as sems, ExitStack() as ctx:
        x = ctx.enter_context(nc.sbuf_tensor("x", [P, NT, H], F32))
        cf = ctx.enter_context(nc.sbuf_tensor("cf", [P, CF_N], F32))
        cb = ctx.enter_context(nc.sbuf_tensor("cb", [P, CB_N], BF16))
        eps = ctx.enter_context(nc.sbuf_tensor("eps", [P, 1], F32))
        zero = ctx.enter_context(nc.sbuf_tensor("zero", [P, 1, H], F32))
        x_rest = sems.enter_context(nc.semaphore("x_rest"))
        x_loaded = sems.enter_context(nc.semaphore("x_loaded"))
        zeroed = sems.enter_context(nc.semaphore("zeroed"))
        cleared = sems.enter_context(nc.semaphore("cleared"))
        pool_dmas = [(sems.enter_context(nc.semaphore(f"scattered_{tag}")),
                      [sems.enter_context(nc.semaphore(f"stored_{tag}_{i}")) for i in range(LB)],
                      [sems.enter_context(nc.semaphore(f"fetched_{tag}_{i}")) for i in range(RB)]) for tag in ("f1", "f2")]
        with nc.Block() as block:
            @block.sync
            def _(sp):
                sp.dma_start(cf[:, :], cf_in).then_inc(x_loaded, 16)
                sp.dma_start(x[:, 0:QT, :], x_in[:, 0:QT, :]).then_inc(x_loaded, 16)
                sp.dma_start(cb[:, 0:CB_SEL], cb_in[:, 0:CB_SEL]).then_inc(x_loaded, 16)
                sp.wait_ge(zeroed, 1)
                sp.dma_start(xs[E * CAP:ROWS].rearrange(token_major, p=P),
                             zero[:, :, :].to_broadcast([P, SPARE, H])).then_inc(cleared, 16)
                sp.wait_ge(x_loaded, 48)

            @block.vector
            def _(dve):
                nc.vector.memset(eps[:, :], EPS)
                nc.vector.memset(zero[:, :, :], 0.0).then_inc(zeroed, 1)
        def router(keep, tag, pool_dmas):
            return Router(nc, sems, keep, tag, x, cf, eps, zero, xs, pool_dmas[0])

        with ExitStack() as keep1, ExitStack() as keep2:
            way1 = router(keep1, "f1", pool_dmas[0])
            way2 = router(keep2, "f2", pool_dmas[1])
            with nc.Block() as block:
                @block.sync
                def _(sp):
                    for way in (way1, way2):
                        sp.dma_start(way.router[:, :, :], ffn_in[0].rearrange("(c p) e -> p c e", p=P)).then_inc(way.router_in, 16)
                    sp.wait_ge(cleared, 16)
            with ExitStack() as attention_sems:
                rest = [(x[:, QT:2 * QT, :], x_in[:, QT:2 * QT, :]), (x[:, 2 * QT:, :], x_in[:, 2 * QT:, :]),
                        (cb[:, CB_SEL:], cb_in[:, CB_SEL:])]
                used = build_attention(nc, attention_sems, x, cf, cb, attention_in, eps, way1, rest, x_rest)
                with nc.Block() as block:
                    @block.gpsimd
                    def _(pool):
                        for s in used:
                            pool.sem_clear(s)
            build_ffn(nc, sems, "f1", cf, ffn_in, xs, ys, way1, pool_dmas[0][1])
            build_mamba(nc, sems, x, cf, cb, mamba_in, eps, ys, way1, pool_dmas[0][2], way2)
            build_ffn(nc, sems, "f2", cf, ffn_in, xs, ys, way2, pool_dmas[1][1])
            build_combine(nc, sems, "f2", x, ys, way2, pool_dmas[1][2], x_out)


def _tables(np, bf16):
    i = np.arange(P)
    cf = np.zeros((P, CF_N), np.float32)
    cf[:, CF_ID:CF_ID + P] = np.eye(P)
    cf[:, CF_TRI:CF_TRI + P] = i[:, None] < i[None, :]
    cf[:, CF_ONE:CF_ONE + P] = 1
    cf[:, CF_IOTA:CF_IOTA + QT * E] = np.tile(np.arange(E) - E, QT)
    cf[:, CF_FRESH:CF_FRESH + QT * E] = np.tile(np.arange(QT) > 0, E)
    cf[:, CF_REGION:CF_REGION + E] = np.arange(E) * CAP
    cf[:, CF_PART] = i
    cf[:, CF_TB:CF_TB + MTILES * E] = np.repeat(np.arange(MTILES) * P, E)
    cb = np.zeros((P, CB_N), bf16)
    cb[:, CB_ID:CB_ID + P] = np.eye(P)
    cb[:, CB_MT:CB_MT + P] = np.where(i[:, None] > i[None, :], MASKED, 0)
    cb[:, CB_MR:CB_MR + P] = np.where(i[None, :] > i[:, None], MASKED, 0)
    for r in range(BCR):
        for s in range(SPLITS):
            cb[s * BCR + r, CB_SEL + r * P:CB_SEL + (r + 1) * P] = 1
    return cf, cb


def kernel(**inputs):
    import ml_dtypes as _ml
    import numpy as _np
    import concourse.bacc as _bacc
    from concourse import mybir as _mybir
    from concourse.bass_utils import run_bass_kernel_spmd as _run

    a = {k: _np.asarray(v) for k, v in inputs.items()}

    def by_half(v):
        return v.reshape(HC, P).T

    at = {k: a["L0_attn_a_" + k] for k in ("Wq", "bq", "Wk", "bk", "Wv", "bv", "Wo", "bo")}
    ma = {k: a["L0_attn_b_" + k] for k in ("conv_w", "conv_b", "x_proj_dt_w", "dt_proj_w", "dt_proj_b",
                                           "B_proj_w", "C_proj_w", "A_log", "D_param")}
    cf, cb = _tables(_np, _ml.bfloat16)
    attention = {k: at[k].T for k in ("Wq", "Wk", "Wv", "Wo")}
    attention.update(bqk=_np.concatenate([at["bq"], at["bk"]]).reshape(2 * HC, P).T, bv=at["bv"], bo=at["bo"])
    mamba = {
        "conv_w": ma["conv_w"][:, 0], "conv_b": by_half(ma["conv_b"]), "x_proj_dt_w": ma["x_proj_dt_w"].T,
        "dt_proj_w": ma["dt_proj_w"].T, "dt_proj_b": by_half(ma["dt_proj_b"]),
        "BC_proj_w": _np.concatenate([ma["B_proj_w"], ma["C_proj_w"]] * SPLITS, 0).T,
        "A_log": ma["A_log"], "D_param": by_half(ma["D_param"]),
    }
    ffn = {k: a["L0_ffn_" + k] for k in ("router_w", "w1", "w3", "w2")}

    nc = _bacc.Bacc("TRN2", target_bir_lowering=False, num_devices=1)
    arrays = {}

    def dram(name, v):
        v = _np.ascontiguousarray(v)
        arrays[f"in_{name}_dram"] = v
        return nc.dram_tensor(f"in_{name}_dram", v.shape, _mybir.dt.from_np(v.dtype), kind="ExternalInput").ap()

    hidden_in = dram("hidden", a["L0_attn_a_hidden_states"])
    cf_in, cb_in = dram("cf", cf), dram("cb", cb)
    attention_in = {k: dram(k, v) for k, v in attention.items()}
    mamba_in = {k: dram(k, v) for k, v in mamba.items()}
    ffn_in = [dram(k, v) for k, v in ffn.items()]
    out = nc.dram_tensor("out_0_dram", (B, S, H), _mybir.dt.from_np(_np.dtype("float32")), kind="ExternalOutput").ap()
    build_layers(nc, hidden_in, cf_in, cb_in, attention_in, mamba_in, ffn_in, out)
    r = _run(nc, [arrays], core_ids=[0])
    return r.results[0]["out_0_dram"]
```
